# Optimizing a Trainium2 kernel written in Bass

```python
import numpy as np
import jax
import jax.numpy as jnp

def _softmax(x, axis=-1):
    return jax.nn.softmax(x, axis=axis)

def _gelu(x):
    return jax.nn.gelu(x, approximate=True)

def _silu(x):
    return jax.nn.silu(x)

def _sigmoid(x):
    return jax.nn.sigmoid(x)

def _layernorm(x, axis=-1, eps=1e-05):
    m = jnp.mean(x, axis=axis, keepdims=True)
    v = jnp.var(x, axis=axis, keepdims=True)
    return (x - m) / jnp.sqrt(v + eps)

def _scatter_add(tgt, idx, src, axis=0):
    return tgt.at[idx].add(src)

def _segment_sum(src, seg, n):
    return jax.ops.segment_sum(src, seg, n)
kernel_name = 'mk_adj_resnorm_d4_adj_r2_913527'

def setup_inputs(seed: int=0):
    np.random.seed(seed)
    _w = jnp.asarray

    def _rec_inputs():
        import jax
        import jax.numpy as jnp
        _gk = jax.random.key(seed)
        x = -0.0002928 + 1 * jax.random.normal(jax.random.fold_in(_gk, 1), (128, 128, 128), jnp.float32)
        _a = jax.random.bernoulli(jax.random.fold_in(_gk, 2), 0.0625, (128, 128, 128))
        _a = jnp.logical_or(_a, jnp.swapaxes(_a, -1, -2))
        _a = jnp.logical_or(_a, jnp.eye(128, dtype=bool))
        _af = _a.astype(jnp.float32)
        _af = _af * jax.random.uniform(jax.random.fold_in(_gk, 3), (128, 128, 128), jnp.float32, 0.05, 4.42607)
        adj = _af
        return (x, adj)
    x, adj = _rec_inputs()

    def _L0_gnn_setup():
        import math
        import jax, jax.numpy as jnp
        import numpy as np
        B, N, D, H = (32, 256, 128, 8)
        HD = D // H
        key = jax.random.key(seed)
        ks = jax.random.split(key, 9)
        h = jax.random.normal(ks[0], (B, N, D), dtype=jnp.float32)
        edge = jax.random.normal(ks[1], (B, N, N), dtype=jnp.float32)
        adj = jax.random.uniform(ks[2], (B, N, N)) < 0.5
        adj_mask = adj | jnp.eye(N, dtype=bool)[None]
        s = 1.0 / math.sqrt(D)
        W_q = jax.random.normal(ks[3], (D, D), dtype=jnp.float32) * s
        W_k = jax.random.normal(ks[4], (D, D), dtype=jnp.float32) * s
        W_v = jax.random.normal(ks[5], (D, D), dtype=jnp.float32) * s
        W_e = jax.random.normal(ks[6], (H, 1), dtype=jnp.float32)
        W_o = jax.random.normal(ks[7], (D, D), dtype=jnp.float32) * s
        return {'h': h, 'edge': edge, 'adj_mask': adj_mask, 'W_q': W_q, 'W_k': W_k, 'W_v': W_v, 'W_e': W_e, 'W_o': W_o}
    _L0_gnn_all = _L0_gnn_setup()
    _L0_gnn_in = {k: v for k, v in _L0_gnn_all.items() if k in ('W_q', 'W_k', 'W_v', 'W_e', 'W_o')}
    del _L0_gnn_all

    def _L1_gnn_setup():
        import jax, jax.numpy as jnp
        import numpy as np
        from jax import lax
        DIM = 128
        EPS = 1e-05

        def _bn(h, g, b, m, v):
            scale = g / jnp.sqrt(v + EPS)
            return h * scale[None, :, None] + (b - m * scale)[None, :, None]

        def _conv1d(h, w, pad):
            return lax.conv_general_dilated(h, w, window_strides=(1,), padding=[(pad, pad)], dimension_numbers=('NCH', 'OIH', 'NCH'))
        key = jax.random.key(seed)
        ks = jax.random.split(key, 16)
        bs, n, d = (16, 1024, DIM)
        s = 0.05
        return {'x': jax.random.normal(ks[0], (bs, n, d), jnp.float32), 'mask': jnp.ones((bs, n, n), jnp.float32), 'w_se': jax.random.normal(ks[1], (3, d), jnp.float32) * s, 'b_se': jnp.zeros((3,), jnp.float32), 'conv1_w': jax.random.normal(ks[2], (d, d, 1), jnp.float32) * s, 'bn1_g': jnp.ones((d,), jnp.float32), 'bn1_b': jnp.zeros((d,), jnp.float32), 'bn1_m': jnp.zeros((d,), jnp.float32), 'bn1_v': jnp.ones((d,), jnp.float32), 'conv2_w': jax.random.normal(ks[3], (d, d, 17), jnp.float32) * s, 'bn2_g': jnp.ones((d,), jnp.float32), 'bn2_b': jnp.zeros((d,), jnp.float32), 'bn2_m': jnp.zeros((d,), jnp.float32), 'bn2_v': jnp.ones((d,), jnp.float32), 'w_msg': jax.random.normal(ks[4], (d, d), jnp.float32) * s, 'b_msg': jnp.zeros((d,), jnp.float32), 'w_ih': jax.random.normal(ks[5], (3 * d, 2 * d), jnp.float32) * s, 'b_ih': jnp.zeros((3 * d,), jnp.float32), 'w_hh': jax.random.normal(ks[6], (3 * d, d), jnp.float32) * s, 'b_hh': jnp.zeros((3 * d,), jnp.float32)}
    _L1_gnn_all = _L1_gnn_setup()
    _L1_gnn_in = {k: v for k, v in _L1_gnn_all.items() if k in ('w_se', 'b_se', 'conv1_w', 'bn1_g', 'bn1_b', 'bn1_m', 'bn1_v', 'conv2_w', 'bn2_g', 'bn2_b', 'bn2_m', 'bn2_v', 'w_msg', 'b_msg', 'w_ih', 'b_ih', 'w_hh', 'b_hh')}
    del _L1_gnn_all

    def _L2_gnn_setup():
        import jax, jax.numpy as jnp
        import numpy as np
        B, N, D = (2, 2048, 128)
        key = jax.random.key(seed)
        ks = jax.random.split(key, 6)
        return {'hidden': jax.random.normal(ks[0], (B, N, D), dtype=jnp.float32), 'mask': jax.random.uniform(ks[1], (B, N, N), dtype=jnp.float32), 'W_w': jax.random.normal(ks[2], (D, D), dtype=jnp.float32) * 0.05, 'W_b': jax.random.normal(ks[3], (D,), dtype=jnp.float32) * 0.05, 'a_w': jax.random.normal(ks[4], (2 * D,), dtype=jnp.float32) * 0.05, 'a_b': jax.random.normal(ks[5], (1,), dtype=jnp.float32) * 0.05}
    _L2_gnn_all = _L2_gnn_setup()
    _L2_gnn_in = {k: v for k, v in _L2_gnn_all.items() if k in ('W_w', 'W_b', 'a_w', 'a_b')}
    del _L2_gnn_all

    def _L3_gnn_setup():
        import jax, jax.numpy as jnp
        import numpy as np
        B, N, IN_DIM, OUT_DIM, H = (8, 512, 128, 128, 4)
        D = OUT_DIM // H
        NEG_INF = -9000000000000000.0
        LRELU_SLOPE = 0.2
        key = jax.random.key(seed)
        k1, k2, k3, k4 = jax.random.split(key, 4)
        x = jax.random.normal(k1, (B, N, IN_DIM), dtype=jnp.float32)
        adj = jax.random.randint(k2, (B, N, N), 0, 2).astype(jnp.float32)
        W = jax.random.normal(k3, (IN_DIM, H * D), dtype=jnp.float32) * jnp.sqrt(2.0 / (IN_DIM + H * D))
        a = jax.random.normal(k4, (H, 2 * D), dtype=jnp.float32) * jnp.sqrt(2.0 / (H + 2 * D))
        return {'x': x, 'adj': adj, 'W': W, 'a': a}
    _L3_gnn_all = _L3_gnn_setup()
    _L3_gnn_in = {k: v for k, v in _L3_gnn_all.items() if k in ('W', 'a')}
    del _L3_gnn_all
    return {'x': x, 'adj': adj, 'L0_gnn_W_q': _L0_gnn_in['W_q'], 'L0_gnn_W_k': _L0_gnn_in['W_k'], 'L0_gnn_W_v': _L0_gnn_in['W_v'], 'L0_gnn_W_e': _L0_gnn_in['W_e'], 'L0_gnn_W_o': _L0_gnn_in['W_o'], 'L1_gnn_w_se': _L1_gnn_in['w_se'], 'L1_gnn_b_se': _L1_gnn_in['b_se'], 'L1_gnn_conv1_w': _L1_gnn_in['conv1_w'], 'L1_gnn_bn1_g': _L1_gnn_in['bn1_g'], 'L1_gnn_bn1_b': _L1_gnn_in['bn1_b'], 'L1_gnn_bn1_m': _L1_gnn_in['bn1_m'], 'L1_gnn_bn1_v': _L1_gnn_in['bn1_v'], 'L1_gnn_conv2_w': _L1_gnn_in['conv2_w'], 'L1_gnn_bn2_g': _L1_gnn_in['bn2_g'], 'L1_gnn_bn2_b': _L1_gnn_in['bn2_b'], 'L1_gnn_bn2_m': _L1_gnn_in['bn2_m'], 'L1_gnn_bn2_v': _L1_gnn_in['bn2_v'], 'L1_gnn_w_msg': _L1_gnn_in['w_msg'], 'L1_gnn_b_msg': _L1_gnn_in['b_msg'], 'L1_gnn_w_ih': _L1_gnn_in['w_ih'], 'L1_gnn_b_ih': _L1_gnn_in['b_ih'], 'L1_gnn_w_hh': _L1_gnn_in['w_hh'], 'L1_gnn_b_hh': _L1_gnn_in['b_hh'], 'L2_gnn_W_w': _L2_gnn_in['W_w'], 'L2_gnn_W_b': _L2_gnn_in['W_b'], 'L2_gnn_a_w': _L2_gnn_in['a_w'], 'L2_gnn_a_b': _L2_gnn_in['a_b'], 'L3_gnn_W': _L3_gnn_in['W'], 'L3_gnn_a': _L3_gnn_in['a']}

def reference(x, adj, L0_gnn_W_q, L0_gnn_W_k, L0_gnn_W_v, L0_gnn_W_e, L0_gnn_W_o, L1_gnn_w_se, L1_gnn_b_se, L1_gnn_conv1_w, L1_gnn_bn1_g, L1_gnn_bn1_b, L1_gnn_bn1_m, L1_gnn_bn1_v, L1_gnn_conv2_w, L1_gnn_bn2_g, L1_gnn_bn2_b, L1_gnn_bn2_m, L1_gnn_bn2_v, L1_gnn_w_msg, L1_gnn_b_msg, L1_gnn_w_ih, L1_gnn_b_ih, L1_gnn_w_hh, L1_gnn_b_hh, L2_gnn_W_w, L2_gnn_W_b, L2_gnn_a_w, L2_gnn_a_b, L3_gnn_W, L3_gnn_a):
    import jax
    import jax.numpy as jnp

    def _L0_gnn_ref(h, edge, adj_mask, W_q, W_k, W_v, W_e, W_o):
        import math
        import jax, jax.numpy as jnp
        import numpy as np
        B, N, D, H = (32, 256, 128, 8)
        HD = D // H
        b, n, _ = h.shape
        q = (h @ W_q.T).reshape(b, n, H, HD).transpose(0, 2, 1, 3)
        k = (h @ W_k.T).reshape(b, n, H, HD).transpose(0, 2, 1, 3)
        v = (h @ W_v.T).reshape(b, n, H, HD).transpose(0, 2, 1, 3)
        edge_bias = jnp.einsum('bij,h->bhij', edge, W_e[:, 0])
        scores = jnp.einsum('bhid,bhjd->bhij', q, k) / math.sqrt(HD) + edge_bias
        scores = jnp.where(adj_mask[:, None], scores, -jnp.inf)
        attn = jax.nn.softmax(scores, axis=-1)
        out = jnp.einsum('bhij,bhjd->bhid', attn, v)
        out = out.transpose(0, 2, 1, 3).reshape(b, n, D)
        return out @ W_o.T

    def _L1_gnn_ref(x, mask, w_se, b_se, conv1_w, bn1_g, bn1_b, bn1_m, bn1_v, conv2_w, bn2_g, bn2_b, bn2_m, bn2_v, w_msg, b_msg, w_ih, b_ih, w_hh, b_hh):
        import jax, jax.numpy as jnp
        import numpy as np
        from jax import lax
        DIM = 128
        EPS = 1e-05

        def _bn(h, g, b, m, v):
            scale = g / jnp.sqrt(v + EPS)
            return h * scale[None, :, None] + (b - m * scale)[None, :, None]

        def _conv1d(h, w, pad):
            return lax.conv_general_dilated(h, w, window_strides=(1,), padding=[(pad, pad)], dimension_numbers=('NCH', 'OIH', 'NCH'))
        d = x.shape[-1]
        xc = jnp.transpose(x, (0, 2, 1))
        h = _bn(_conv1d(xc, conv1_w, 0), bn1_g, bn1_b, bn1_m, bn1_v)
        h = jax.nn.relu(h)
        h = _bn(_conv1d(h, conv2_w, 8), bn2_g, bn2_b, bn2_m, bn2_v)
        x_conv = jnp.transpose(jax.nn.relu(h + xc), (0, 2, 1))
        s = x @ w_se.T + b_se
        sq = jnp.sum(s * s, axis=-1)
        dist = sq[:, :, None] + sq[:, None, :] - 2.0 * jnp.einsum('bnd,bmd->bnm', s, s)
        A = jnp.exp(-dist) * mask
        msg = jax.nn.relu(x @ w_msg.T + b_msg)
        x_nmp = jnp.einsum('bnm,bmd->bnd', A, msg)
        x_in = jnp.concatenate([x_conv, x_nmp], axis=-1)
        gi = x_in @ w_ih.T + b_ih
        gh = x @ w_hh.T + b_hh
        gi_r, gi_z, gi_n = (gi[..., :d], gi[..., d:2 * d], gi[..., 2 * d:])
        gh_r, gh_z, gh_n = (gh[..., :d], gh[..., d:2 * d], gh[..., 2 * d:])
        r = jax.nn.sigmoid(gi_r + gh_r)
        z = jax.nn.sigmoid(gi_z + gh_z)
        nn_ = jnp.tanh(gi_n + r * gh_n)
        return (1.0 - z) * nn_ + z * x

    def _L2_gnn_ref(hidden, mask, W_w, W_b, a_w, a_b):
        import jax, jax.numpy as jnp
        import numpy as np
        B, N, D = (2, 2048, 128)
        h = jnp.einsum('bnd,ed->bne', hidden, W_w) + W_b
        Dh = h.shape[-1]
        a1, a2 = (a_w[:Dh], a_w[Dh:])
        e = h @ a1
        f = h @ a2
        logits = e[:, :, None] + f[:, None, :] + a_b[0]
        u = mask * jnp.exp(logits)
        a = u / jnp.sum(u, axis=2, keepdims=True)
        h_prime = jnp.einsum('bnm,bmd->bnd', a, h)
        return h_prime

    def _L3_gnn_ref(x, adj, W, a):
        import jax, jax.numpy as jnp
        import numpy as np
        B, N, IN_DIM, OUT_DIM, H = (8, 512, 128, 128, 4)
        D = OUT_DIM // H
        NEG_INF = -9000000000000000.0
        LRELU_SLOPE = 0.2
        h = jnp.einsum('bni,io->bno', x, W).reshape(x.shape[0], x.shape[1], H, D)
        h = h.transpose(0, 2, 1, 3)
        a1, a2 = (a[:, :D], a[:, D:])
        e_i = jnp.einsum('bhnd,hd->bhn', h, a1)
        e_j = jnp.einsum('bhmd,hd->bhm', h, a2)
        e = e_i[:, :, :, None] + e_j[:, :, None, :]
        e = jnp.where(e > 0, e, LRELU_SLOPE * e)
        e = jnp.where(adj[:, None, :, :] > 0, e, NEG_INF)
        attn = jax.nn.softmax(e, axis=-1)
        out = jnp.einsum('bhnm,bhmd->bhnd', attn, h)
        out = out.transpose(0, 2, 1, 3).reshape(x.shape[0], x.shape[1], H * D)
        return out
    x = _layernorm(x + _L0_gnn_ref(x, adj, adj, L0_gnn_W_q, L0_gnn_W_k, L0_gnn_W_v, L0_gnn_W_e, L0_gnn_W_o), axis=-1)
    x = _layernorm(x + _L1_gnn_ref(x, adj, L1_gnn_w_se, L1_gnn_b_se, L1_gnn_conv1_w, L1_gnn_bn1_g, L1_gnn_bn1_b, L1_gnn_bn1_m, L1_gnn_bn1_v, L1_gnn_conv2_w, L1_gnn_bn2_g, L1_gnn_bn2_b, L1_gnn_bn2_m, L1_gnn_bn2_v, L1_gnn_w_msg, L1_gnn_b_msg, L1_gnn_w_ih, L1_gnn_b_ih, L1_gnn_w_hh, L1_gnn_b_hh), axis=-1)
    x = _layernorm(x + _L2_gnn_ref(x, adj, L2_gnn_W_w, L2_gnn_W_b, L2_gnn_a_w, L2_gnn_a_b), axis=-1)
    x = _layernorm(x + _L3_gnn_ref(x, adj, L3_gnn_W, L3_gnn_a), axis=-1)
    return x

_drawn_inputs = setup_inputs


def setup_inputs(seed=0):
    import zlib

    import numpy as np

    out = dict(_drawn_inputs(seed))
    spreads = {'L1_gnn_b_se': (0.0, 0.8),
     'L1_gnn_bn1_g': (1.0, 0.6),
     'L1_gnn_bn1_b': (0.0, 0.518),
     'L1_gnn_bn1_m': (0.0, 0.486),
     'L1_gnn_bn1_v': (1.0, 0.6),
     'L1_gnn_bn2_g': (1.0, 0.6),
     'L1_gnn_bn2_b': (0.0, 0.8),
     'L1_gnn_bn2_m': (0.0, 0.623),
     'L1_gnn_bn2_v': (1.0, 0.6),
     'L1_gnn_b_msg': (0.0, 0.1),
     'L1_gnn_b_ih': (0.0, 0.301),
     'L1_gnn_b_hh': (0.0, 0.374)}
    factors = {}
    for name, (base, spread) in spreads.items():
        noise = np.random.default_rng([zlib.crc32(name.encode()), seed]).standard_normal(out[name].shape)
        drawn = base * np.exp(spread * noise) if base else spread * noise
        out[name] = jnp.asarray(drawn.astype(out[name].dtype))
    for name, factor in factors.items():
        out[name] = (out[name] * factor).astype(out[name].dtype)
    return out
```

```python
from contextlib import ExitStack

import concourse.bass as bass
from concourse import mybir

F32 = mybir.dt.float32
BF16 = mybir.dt.bfloat16
ALU = mybir.AluOpType
ACT = mybir.ActivationFunctionType
AX = mybir.AxisListType.X

N = 128
GB = 4
W = GB * N
GROUPS = N // GB
H0, D0 = 8, 16
H3, D3 = 4, 32
TAPS, PAD = 17, 8
NP = N + 2 * PAD
EPS = 1e-5
NEG0 = -1.0e30
NEG3 = -9.0e15
SLOPE = 0.2
NS = 3
KS = 3 * NS
HC = N + 2
GC = N + H3
DMA = 16

(C_G1, C_B1, C_M1, C_V1, C_G2, C_B2, C_M2, C_V2, C_BIR, C_BIZ, C_BIN, C_BHR, C_BHZ, C_BHN, C_A1, C_A2,
 C_WB) = range(17)
NCOL = 17
R_WE, R_BM, R_WB, R_AB = 0, H0, H0 + N, H0 + 2 * N
NROW = H0 + 2 * N + 1
WQ, WK, WV, WO, W1, WM, WL2, WL2N, WL3, WL3T, WHH = (N * i for i in range(11))
WIC, WIN, WC2 = N * 13, N * 16, N * 19
NMAT = N * (19 + TAPS)


def build(nc, x_n, x_t, adj_n, adj_t, mats, wse, cols, rows, bse, att3, out):
    with ExitStack() as ctx:
        def sb(name, shape, dt=F32):
            return ctx.enter_context(nc.sbuf_tensor(name, shape, dt))

        def ps(name, shape, dt=F32):
            return ctx.enter_context(nc.psum_tensor(name, shape, dt))

        def sem(name):
            return ctx.enter_context(nc.semaphore(name))

        wm = sb("wm", [128, NMAT])
        col = sb("col", [128, NCOL])
        row = sb("row", [1, NROW])
        wse_s = sb("wse_s", [128, KS])
        bse_s = sb("bse_s", [KS, 1])
        att = sb("att", [128, 2 * H3])
        ident = sb("ident", [128, 128])
        identb = sb("identb", [128, 128], BF16)
        ones = sb("ones", [128, 128])
        headm = sb("headm", [128, H0])
        sel = sb("sel", [KS, 4])
        sel2 = sb("sel2", [KS, 1])
        neghalf = sb("neghalf", [128, GB])
        eps4 = sb("eps4", [128, GB])
        bns = sb("bns", [128, 2])
        bnt = sb("bnt", [128, 2])
        bnb = sb("bnb", [128, 2])
        gb = sb("gb", [128, 2])
        rowb = sb("rowb", [128, H0 + 2 * N + 2])
        brow = sb("brow", [1, 2])
        l2w = sb("l2w", [128, HC])
        l3w = sb("l3w", [128, GC])
        wa2 = sb("wa2", [128, H3])
        wa2b = sb("wa2b", [128, H3, 128])
        we = rowb[:, 0:H0]
        bmsg = rowb[:, H0:H0 + N]
        bl2 = rowb[:, H0 + N:H0 + 2 * N + 2]

        xn = [sb(f"xn{p}", [128, W]) for p in range(2)]
        xt = [sb(f"xt{p}", [128, W]) for p in range(2)]
        an = [sb(f"an{p}", [128, W]) for p in range(2)]
        at = [sb(f"at{p}", [128, W]) for p in range(2)]
        mask3 = [sb(f"mask3{p}", [128, W], BF16) for p in range(2)]
        mask0 = sb("mask0", [128, W], BF16)
        qT = sb("qT", [128, W])
        kT = sb("kT", [128, W])
        kh = sb("kh", [128, H0, W])
        vpad = sb("vpad", [128, GB * H0 * 32])
        sc0 = sb("sc0", [128, 2, W])
        nm0 = sb("nm0", [128, 2, GB])
        e0 = sb("e0", [128, 2, W])
        sum0 = sb("sum0", [128, 2, GB])
        rec0 = sb("rec0", [128, 2, GB])
        p0 = sb("p0", [128, 2, W])
        pT0 = sb("pT0", [128, 2, W])
        oT = sb("oT", [128, W])
        r0 = sb("r0", [128, W])
        x1 = sb("x1", [128, W])
        x1T = sb("x1T", [128, W])
        hp = sb("hp", [128, GB, NP])
        dd = sb("dd", [KS, W])
        sql = sb("sql", [KS, W])
        sqr = sb("sqr", [KS, W])
        ll = sb("ll", [KS, W])
        lr = sb("lr", [KS, W])
        m1 = sb("m1", [128, W])
        msg = sb("msg", [128, W])
        em = sb("em", [128, W])
        aT = sb("aT", [128, W])
        u1 = sb("u1", [128, W])
        xcT = sb("xcT", [128, W])
        nmT = sb("nmT", [128, W])
        tr = sb("tr", [128, W])
        tz = sb("tz", [128, W])
        rr = sb("rr", [128, W])
        g1 = sb("g1", [128, W])
        g2 = sb("g2", [128, W])
        nT = sb("nT", [128, W])
        dx = sb("dx", [128, W])
        nx = sb("nx", [128, W])
        zd = sb("zd", [128, W])
        yT = sb("yT", [128, W])
        x2 = sb("x2", [128, W])
        x2T = sb("x2T", [128, W])
        h2 = sb("h2", [128, GB, HC])
        eg = sb("eg", [128, GB, 2])
        hg = sb("hg", [128, GB, HC])
        dn = sb("dn", [128, GB])
        rdn = sb("rdn", [128, GB])
        wr = sb("wr", [128, GB])
        r2 = sb("r2", [128, W])
        x3 = sb("x3", [128, W])
        x3T = sb("x3T", [128, W])
        h3 = sb("h3", [128, GB, GC])
        z3 = sb("z3", [128, 2, W])
        l3 = sb("l3", [128, 2, W])
        nm3 = sb("nm3", [128, 2, GB])
        e3 = sb("e3", [128, 2, W])
        sum3 = sb("sum3", [128, 2, GB])
        rec3 = sb("rec3", [128, 2, GB])
        p3 = sb("p3", [128, 2, W])
        pT3 = sb("pT3", [128, 2, W])
        o3T = sb("o3T", [128, W])
        r3 = sb("r3", [128, W])
        xo = [sb(f"xo{p}", [128, W]) for p in range(2)]
        stats = [sb(f"stats{i}", [128, GB, 6]) for i in range(4)]
        meanv = [sb(f"meanv{i}", [128, GB, 2]) for i in range(4)]
        veps = [sb(f"veps{i}", [128, GB]) for i in range(4)]
        rstd = [sb(f"rstd{i}", [128, GB]) for i in range(4)]

        S = [ps("S0", [128, W]), ps("S1", [128, W])]
        T = ps("T", [128, W])
        O = ps("O", [128, W])
        J = ps("J", [128, W])
        B = ps("B", [128, 3, W])

        names = """wload wcol ones_set pads_set sel_set id_set const_set bn1_ bn2_ bn3_ bn4_ rows_ps rowb_set
            brow_ps brow_set bl2_ps bl2_set wa_ps wa_set wa2b_set prep
            q_ps k_ps v_ps qT_ready kT_ready v_ready mask0_ready mask3_ready oT_ready wo_ps res0_done
            x1t_ps x1T_ready c1_ps hp_ready d_ps dd_ready sq_ready lr_done msg_ps m1_done msg_ready c2_ps
            u_done xc_ready arg_ps em_ready aT_done nmp_ps nmT_ready ghn_ps r_ps tr_ready z_ps tz_ready
            gin_ps rr_done g1_done g2_done n_ready dx_done zd_done y_done yt_ps
            x2t_ps x2T_ready h2_ps hb_done eg_ready hg_done num_ps dn_done rdn_done wr_done r2_done
            x3t_ps x3T_ready h3_ps h3_ready o3T_ready o3n_ps r3_done""".split()
        per_head = """kh_ready qk_ps sc_ready nm_ready exp_done rec_done p_ready tr_ps pT_ready pv_ps
            e3_ps z3_ready l3_done nm3_ready exp3_done rec3_done p3_ready tr3_ps pT3_ready pv3_ps""".split()
        q = {n: sem(n) for n in names + per_head}
        loaded = [sem("loaded0"), sem("loaded1")]
        stored = [sem("stored0"), sem("stored1")]
        ln_stats = [sem(f"ln_stats{i}") for i in range(4)]
        ln_aggr = [sem(f"ln_aggr{i}") for i in range(4)]
        ln_veps = [sem(f"ln_veps{i}") for i in range(4)]
        ln_rstd = [sem(f"ln_rstd{i}") for i in range(4)]
        ln_out = [sem(f"ln_out{i}") for i in range(4)]

        def g(t, b):
            return t[:, b * N:(b + 1) * N]

        def per(t):
            return t.rearrange("p (b n) -> p b n", b=GB)

        def wide(s):
            return s.unsqueeze(2).broadcast_to([128, GB, N])

        def wait(eng, s, value):
            if isinstance(value, int) and value <= 0:
                return
            eng.wait_ge(s, value)

        def steps(eng, step):
            step(0, 0, True, False)
            step(0, 1, True, True)
            with eng.Fori(1, GROUPS // 2) as k:
                step(k, 0, True, True)
                step(k, 1, True, True)
            step(GROUPS // 2, 0, False, True)

        block = ctx.enter_context(nc.Block())

        @block.sync
        def _(sp):
            def load(k, p):
                s = 2 * k + p
                for dst, src in ((xt, x_t), (an, adj_n), (xn, x_n), (at, adj_t)):
                    sp.dma_start(dst[p][:, :], src[:, bass.ds(s * W, W)]).then_inc(loaded[p], DMA)

            def store(k, p):
                s = 2 * k + p
                wait(sp, ln_out[3], s + 1)
                sp.dma_start(out[:, bass.ds(s * W, W)], xo[p][:, :]).then_inc(stored[p], DMA)

            sp.dma_start(wm[:, 0:WIC], mats[:, 0:WIC]).then_inc(q["wload"], DMA)
            load(0, 0)
            sp.dma_start(col[:, :], cols).then_inc(q["wcol"], DMA)
            sp.dma_start(row[:, :], rows).then_inc(q["wcol"], DMA)
            sp.dma_start(wse_s[:, :], wse).then_inc(q["wcol"], DMA)
            sp.dma_start(bse_s[:, :], bse).then_inc(q["wcol"], DMA)
            sp.wait_ge(q["pads_set"], 1)
            for h in range(H3):
                for j in range(2):
                    sp.dma_start(att[h * D3:(h + 1) * D3, j * H3 + h:j * H3 + h + 1],
                                 att3[h, j * D3:(j + 1) * D3].rearrange("(d o) -> d o", o=1))\
                        .then_inc(q["wcol"], DMA)
            sp.dma_start(wm[:, WIC:NMAT], mats[:, WIC:NMAT]).then_inc(q["wload"], DMA)
            load(0, 1)
            with sp.Fori(0, GROUPS // 2 - 1) as k:
                for p in range(2):
                    s = 2 * k + p
                    sp.wait_ge(q["v_ps"], s + 1)
                    sp.wait_ge(q["res0_done"], s + 1)
                    sp.wait_ge(q["mask3_ready"], s + 1)
                    sp.wait_ge(q["num_ps"], s + 1)
                    load(k + 1, p)
                    store(k, p)
            store(GROUPS // 2 - 1, 0)
            store(GROUPS // 2 - 1, 1)
            sp.wait_ge(stored[0], DMA * GROUPS // 2)
            sp.wait_ge(stored[1], DMA * GROUPS // 2)

        @block.gpsimd
        def _(pool):
            pool.memset(ones[:, :], 1.0).then_inc(q["ones_set"], 1)
            pool.memset(att[:, :], 0.0)
            pool.memset(hp[:, :, :], 0.0)
            pool.memset(neghalf[:, :], -0.5)
            pool.memset(eps4[:, :], EPS)
            pool.memset(vpad[:, :], 0.0).then_inc(q["pads_set"], 1)
            pool.memset(sel[:, :], 1.0)
            pool.memset(ident[:, :], 0.0).then_inc(q["sel_set"], 1)
            pool.memset(headm[:, :], 1.0).then_inc(q["sel_set"], 1)
            pool.wait_ge(q["sel_set"], 2)
            pool.affine_select(out=ident[:, :], in_=ident[:, :], compare_op=ALU.not_equal, fill=1.0, base=0,
                               pattern=[[-1, 128]], channel_multiplier=1).then_inc(q["id_set"], 1)
            pool.affine_select(out=headm[:, :], in_=headm[:, :], compare_op=ALU.is_ge, fill=0.0, base=0,
                               pattern=[[-D0, H0]], channel_multiplier=1).then_inc(q["id_set"], 1)
            pool.affine_select(out=sel[:, :], in_=sel[:, :], compare_op=ALU.is_ge, fill=0.0, base=0,
                               pattern=[[-NS, 4]], channel_multiplier=1).then_inc(q["id_set"], 1)
            pool.wait_ge(q["id_set"], 3)
            pool.affine_select(out=headm[:, :], in_=headm[:, :], compare_op=ALU.is_ge, fill=0.0, base=D0 - 1,
                               pattern=[[D0, H0]], channel_multiplier=-1).then_inc(q["const_set"], 1)
            pool.affine_select(out=sel[:, :], in_=sel[:, :], compare_op=ALU.is_ge, fill=0.0, base=NS - 1,
                               pattern=[[NS, 4]], channel_multiplier=-1).then_inc(q["const_set"], 1)
            pool.tensor_copy(identb[:, :], ident[:, :]).then_inc(q["const_set"], 1)
            pool.wait_ge(q["const_set"], 2)
            pool.tensor_scalar(sel2[:, :], sel[:, 0:1], 2.0, 1.0, ALU.mult, ALU.mult).then_inc(q["const_set"], 1)
            pool.wait_ge(q["wcol"], 12 * DMA)
            pool.wait_ge(q["const_set"], 4)
            for j, v in enumerate((C_V1, C_V2)):
                pool.tensor_scalar(bnt[:, j:j + 1], col[:, v:v + 1], EPS, 1.0, ALU.add, ALU.mult)\
                    .then_inc(q["bn1_"], 1)
            pool.wait_ge(q["bn1_"], 2)
            pool.tensor_tensor(bns[:, :], bnt[:, :], neghalf[:, 0:2], ALU.pow).then_inc(q["bn2_"], 1)

            def rsqrt(i, u):
                pool.wait_ge(ln_aggr[i], u + 1)
                pool.tensor_tensor(veps[i][:, :], meanv[i][:, :, 1], eps4[:, :], ALU.add)\
                    .then_inc(ln_veps[i], 1)
                pool.wait_ge(ln_veps[i], u + 1)
                pool.tensor_tensor(rstd[i][:, :], veps[i][:, :], neghalf[:, :], ALU.pow)\
                    .then_inc(ln_rstd[i], 1)

            def k_heads(s):
                wait(pool, q["wo_ps"], s)
                pool.wait_ge(q["kT_ready"], s + 1)
                pool.tensor_tensor(kh[:, 0, :], kT[:, :], headm[:, 0:1].broadcast_to([128, W]), ALU.mult)\
                    .then_inc(q["kh_ready"], 1)
                for h in range(1, H0):
                    pool.tensor_scalar(kh[:, h, :], kT[:, :], headm[:, h:h + 1], 1.0, ALU.mult, ALU.mult)\
                        .then_inc(q["kh_ready"], 1)

            def step(k, p, front, back):
                s = 2 * k + p
                u = s - 1
                if front:
                    k_heads(s)
                if back:
                    pool.wait_ge(loaded[1 - p], (k + p) * 4 * DMA)
                    pool.wait_ge(q["em_ready"], u + 1)
                    wait(pool, q["nmp_ps"], u)
                    pool.tensor_tensor(aT[:, :], em[:, :], at[1 - p][:, :], ALU.mult).then_inc(q["aT_done"], 1)
                    pool.wait_ge(q["n_ready"], u + 1)
                    wait(pool, q["y_done"], u)
                    pool.tensor_tensor(dx[:, :], x1T[:, :], nT[:, :], ALU.subtract)
                    pool.tensor_tensor(nx[:, :], x1T[:, :], nT[:, :], ALU.add).then_inc(q["dx_done"], 1)
                    rsqrt(1, u)
                if front and not back:
                    rsqrt(0, s)
                if back:
                    rsqrt(2, u)
                    if front:
                        rsqrt(0, s)
                    rsqrt(3, u)

            steps(pool, step)

        @block.tensor
        def _(pe):
            mm = nc.tensor.matmul

            pe.wait_ge(q["ones_set"], 1)
            pe.wait_ge(q["wcol"], 12 * DMA)
            pe.wait_ge(q["wload"], 2 * DMA)
            mm(B[:, 0, 0:NROW - 1], ones[0:1, :], row[:, 0:NROW - 1], start=True, stop=True)\
                .then_inc(q["rows_ps"], 1)
            mm(B[0:1, 1, 0:2], col[:, C_WB:C_WB + 1], col[:, C_A1:C_A2 + 1], start=True, stop=True)\
                .then_inc(q["brow_ps"], 1)
            mm(B[:, 2, 0:2], wm[:, WL2N:WL2N + N], col[:, C_A1:C_A2 + 1], start=True, stop=True)
            mm(S[0][:, 0:2 * H3], wm[:, WL3T:WL3T + N], att[:, :], start=True, stop=True).then_inc(q["wa_ps"], 1)
            pe.wait_ge(q["brow_set"], 1)
            mm(S[1][:, 0:2], ones[0:1, :], brow[:, :], start=True, stop=True).then_inc(q["bl2_ps"], 1)
            pe.wait_ge(q["prep"], 1)

            def transpose4(dst, src):
                for b in range(GB):
                    last = nc.tensor.transpose(g(dst, b), g(src, b), ident[:, :])
                return last

            def project(s, p, k):
                pe.wait_ge(loaded[p], (k + 1) * 4 * DMA)
                wait(pe, q["res0_done"], s)
                mm(J[:, :], wm[:, WQ:WQ + N], xt[p][:, :], start=True, stop=True).then_inc(q["q_ps"], 1)
                wait(pe, q["pT_ready"], 8 * s)
                mm(T[:, :], wm[:, WK:WK + N], xt[p][:, :], start=True, stop=True).then_inc(q["k_ps"], 1)
                wait(pe, q["oT_ready"], s)
                for b in range(GB):
                    last = mm(g(O, b), g(xt[p], b), wm[:, WV:WV + N], start=True, stop=True)
                last.then_inc(q["v_ps"], 1)

            def scores(s, h):
                if h == 0:
                    pe.wait_ge(q["mask0_ready"], s + 1)
                    pe.wait_ge(q["qT_ready"], s + 1)
                pe.wait_ge(q["kh_ready"], 8 * s + h + 1)
                wait(pe, q["sc_ready"], 8 * s + h - 1)
                mm(S[h % 2][:, :], identb[:, :], mask0[:, :], start=True, stop=False, skip_group_check=True)
                for b in range(GB):
                    last = mm(g(S[h % 2], b), g(qT, b), g(kh[:, h, :], b), start=False, stop=True,
                              skip_group_check=True)
                last.then_inc(q["qk_ps"], 1)

            def probs_T(s, h):
                pe.wait_ge(q["p_ready"], 8 * s + h + 1)
                wait(pe, q["pT_ready"], 8 * s + h)
                if h == 0:
                    pe.wait_ge(q["kT_ready"], s + 1)
                transpose4(T, p0[:, h % 2, :]).then_inc(q["tr_ps"], 1)

            def values(s, h):
                pe.wait_ge(q["pT_ready"], 8 * s + h + 1)
                if h == 0:
                    pe.wait_ge(q["v_ready"], s + 1)
                r = slice(32 * (h // 2), 32 * (h // 2) + 32)
                for b in range(GB):
                    c = (b * H0 + h) * 32
                    last = mm(O[r, b * N:(b + 1) * N], vpad[:, c:c + 32], g(pT0[:, h % 2, :], b),
                              start=(h % 2 == 0 and b == 0), stop=(h % 2 == 1), skip_group_check=True)
                last.then_inc(q["pv_ps"], 1)

            def project_out(s):
                pe.wait_ge(q["oT_ready"], s + 1)
                for b in range(GB):
                    last = mm(g(J, b), g(oT, b), wm[:, WO:WO + N], start=True, stop=True)
                last.then_inc(q["wo_ps"], 1)

            def conv_taps(u, a, z):
                if a == 0:
                    pe.wait_ge(q["hp_ready"], u + 1)
                for t in range(a, z):
                    last = mm(per(B[:, 1, :]), wm[:, WC2 + t * N:WC2 + (t + 1) * N], hp[:, :, t:t + N],
                              start=(t == 0), stop=(t == TAPS - 1), skip_group_check=True)
                if z == TAPS:
                    last.then_inc(q["c2_ps"], 1)

            def back_slot(u, i):
                if i == 0:
                    pe.wait_ge(ln_out[0], u + 1)
                    wait(pe, q["o3T_ready"], u)
                    transpose4(B[:, 0, :], x1).then_inc(q["x1t_ps"], 1)
                if i == 1:
                    pe.wait_ge(q["x1T_ready"], u + 1)
                    wait(pe, q["r3_done"], u)
                    mm(B[:, 1, :], wm[:, W1:W1 + N], x1T[:, :], start=True, stop=True).then_inc(q["c1_ps"], 1)
                    wait(pe, q["z3_ready"], H3 * u)
                    mm(B[0:KS, 2, :], wse_s[:, :], x1T[:, :], start=True, stop=True).then_inc(q["d_ps"], 1)
                    for b in range(GB):
                        last = mm(g(B[:, 0, :], b), g(x1T, b), wm[:, WM:WM + N], start=True, stop=True)
                    last.then_inc(q["msg_ps"], 1)
                if i == 2:
                    conv_taps(u, 0, 6)
                    pe.wait_ge(q["lr_done"], u + 1)
                    for b in range(GB):
                        last = mm(g(B[:, 2, :], b), g(ll, b), g(lr, b), start=True, stop=True)
                    last.then_inc(q["arg_ps"], 1)
                if i == 3:
                    conv_taps(u, 6, 11)
                if i == 4:
                    conv_taps(u, 11, TAPS)
                    pe.wait_ge(q["aT_done"], u + 1)
                    pe.wait_ge(q["msg_ready"], u + 1)
                    for b in range(GB):
                        last = mm(g(B[:, 0, :], b), g(msg, b), g(aT, b), start=True, stop=True)
                    last.then_inc(q["nmp_ps"], 1)
                if i == 5:
                    def gate(bank, j, parts, done):
                        for n, (w, src) in enumerate(parts):
                            last = mm(B[:, bank, :], wm[:, w + j * N:w + (j + 1) * N], src[:, :],
                                      start=(n == 0), stop=(n == len(parts) - 1))
                        last.then_inc(q[done], 1)
                    pe.wait_ge(q["nmT_ready"], u + 1)
                    pe.wait_ge(q["xc_ready"], u + 1)
                    pe.wait_ge(q["em_ready"], u + 1)
                    gate(2, 0, [(WHH, x1T), (WIC, xcT), (WIN, nmT)], "r_ps")
                    gate(0, 2, [(WHH, x1T)], "ghn_ps")
                    gate(1, 1, [(WHH, x1T), (WIC, xcT), (WIN, nmT)], "z_ps")
                    pe.wait_ge(q["tr_ready"], u + 1)
                    gate(2, 2, [(WIC, xcT), (WIN, nmT)], "gin_ps")
                if i == 7:
                    pe.wait_ge(q["y_done"], u + 1)
                    transpose4(B[:, 1, :], yT).then_inc(q["yt_ps"], 1)
                if i == 8:
                    pe.wait_ge(ln_out[1], u + 1)
                    transpose4(B[:, 0, :], x2).then_inc(q["x2t_ps"], 1)
                    pe.wait_ge(q["x2T_ready"], u + 1)
                    for b in range(GB):
                        c = (b % 2) * HC
                        last = mm(B[:, 1 + b // 2, c:c + HC], g(x2T, b), l2w[:, :], start=True, stop=True)
                    last.then_inc(q["h2_ps"], 1)
                if i == 9:
                    pe.wait_ge(q["hg_done"], u + 1)
                    for b in range(GB):
                        c = (b % 2) * HC
                        last = mm(B[:, b // 2, c:c + HC], g(at[1 - PAR[0]], b), hg[:, b, :], start=True, stop=True)
                    last.then_inc(q["num_ps"], 1)
                if i == 11:
                    pe.wait_ge(ln_out[2], u + 1)
                    transpose4(B[:, 2, :], x3).then_inc(q["x3t_ps"], 1)
                    pe.wait_ge(q["x3T_ready"], u + 1)
                    for b in range(GB):
                        c = (b % 2) * GC
                        last = mm(B[:, b // 2, c:c + GC], g(x3T, b), l3w[:, :], start=True, stop=True)
                    last.then_inc(q["h3_ps"], 1)
                    pe.wait_ge(q["mask3_ready"], u + 1)
                if 11 <= i < 11 + H3:
                    h = i - 11
                    wait(pe, q["z3_ready"], H3 * u + h)
                    mm(B[:, 2, :], wa2b[:, h, :], x3T[:, :], start=True, stop=False)
                    mm(B[:, 2, :], identb[:, :], mask3[1 - PAR[0]][:, :], start=False, stop=True)\
                        .then_inc(q["e3_ps"], 1)
                if 12 <= i < 12 + H3:
                    h = i - 12
                    pe.wait_ge(q["p3_ready"], H3 * u + h + 1)
                    wait(pe, q["pT3_ready"], H3 * u + h)
                    if h == 0:
                        pe.wait_ge(q["h3_ready"], u + 1)
                    transpose4(B[:, 1, :], p3[:, h % 2, :]).then_inc(q["tr3_ps"], 1)
                    pe.wait_ge(q["pT3_ready"], H3 * u + h + 1)
                    for b in range(GB):
                        last = mm(B[32 * h:32 * h + 32, 0, b * N:(b + 1) * N], h3[:, b, h * D3:(h + 1) * D3],
                                  g(pT3[:, h % 2, :], b), start=(b == 0), stop=True, skip_group_check=True)
                    last.then_inc(q["pv3_ps"], 1)
                if i == 12 + H3:
                    pe.wait_ge(q["o3T_ready"], u + 1)
                    transpose4(B[:, 1, :], o3T).then_inc(q["o3n_ps"], 1)

            PAR = [0]

            def step(k, p, front, back):
                s = 2 * k + p
                u = s - 1
                PAR[0] = p
                for i in range(SLOTS):
                    if front:
                        if i == 0:
                            project(s, p, k)
                        if 0 <= i - 1 < H0:
                            scores(s, i - 1)
                        if 0 <= i - 3 < H0:
                            values(s, i - 3)
                    if back:
                        back_slot(u, i)
                    if front:
                        if 0 <= i - 2 < H0:
                            probs_T(s, i - 2)
                        if i == H0 + 3:
                            project_out(s)

            steps(pe, step)

        @block.scalar
        def _(act):
            fn = nc.scalar.activation

            def project(s, p, k):
                act.wait_ge(q["q_ps"], s + 1)
                wait(act, q["qk_ps"], 8 * s)
                fn(qT[:, :], J[:, :], ACT.Copy, scale=float(D0) ** -0.5).then_inc(q["qT_ready"], 1)
                act.wait_ge(q["k_ps"], s + 1)
                wait(act, q["kh_ready"], 8 * s)
                fn(kT[:, :], T[:, :], ACT.Copy).then_inc(q["kT_ready"], 1)
                act.wait_ge(q["v_ps"], s + 1)
                wait(act, q["pv_ps"], 8 * s)
                src = O[:, :].rearrange("p (m e d) -> p m e d", e=2, d=D0)
                dst = vpad[:, :].rearrange("p (m e f d) -> p m e f d", e=2, f=2, d=D0)
                fn(dst[:, :, 0, 0, :], src[:, :, 0, :], ACT.Copy)
                fn(dst[:, :, 1, 1, :], src[:, :, 1, :], ACT.Copy).then_inc(q["v_ready"], 1)

            def exps(s, h):
                act.wait_ge(q["nm_ready"], 8 * s + h + 1)
                wait(act, q["p_ready"], 8 * s + h - 1)
                for b in range(GB):
                    last = fn(g(e0[:, h % 2, :], b), g(sc0[:, h % 2, :], b), ACT.Exp, bias=nm0[:, h % 2, b:b + 1],
                              accum_out=sum0[:, h % 2, b:b + 1])
                last.then_inc(q["exp_done"], 1)

            def probs_T(s, h):
                act.wait_ge(q["tr_ps"], 8 * s + h + 1)
                wait(act, q["pv_ps"], 8 * s + h - 1)
                fn(pT0[:, h % 2, :], T[:, :], ACT.Copy).then_inc(q["pT_ready"], 1)

            def back_slot(u, i):
                if i == 0:
                    act.wait_ge(q["x1t_ps"], u + 1)
                    wait(act, q["y_done"], u)
                    fn(x1T[:, :], B[:, 0, :], ACT.Copy).then_inc(q["x1T_ready"], 1)
                if i == 1:
                    act.wait_ge(q["c1_ps"], u + 1)
                    wait(act, q["c2_ps"], u)
                    fn(hp[:, :, PAD:PAD + N], per(B[:, 1, :]), ACT.Relu, bias=bnb[:, 0:1], scale=bns[:, 0:1])\
                        .then_inc(q["hp_ready"], 1)
                    act.wait_ge(q["d_ps"], u + 1)
                    wait(act, q["lr_done"], u)
                    fn(dd[:, :], B[0:KS, 2, :], ACT.Identity, bias=bse_s[:, :]).then_inc(q["dd_ready"], 1)
                    act.wait_ge(q["dd_ready"], u + 1)
                    fn(sql[:, :], dd[:, :], ACT.Square, scale=sel[:, 2:3], bias=sel[:, 1:2])
                    fn(sqr[:, :], dd[:, :], ACT.Square, scale=sel[:, 1:2], bias=sel[:, 2:3])\
                        .then_inc(q["sq_ready"], 1)
                    act.wait_ge(q["m1_done"], u + 1)
                    wait(act, q["nmp_ps"], u)
                    fn(msg[:, :], m1[:, :], ACT.Relu).then_inc(q["msg_ready"], 1)
                if i == 2:
                    act.wait_ge(q["arg_ps"], u + 1)
                    wait(act, q["aT_done"], u)
                    fn(em[:, :], B[:, 2, :], ACT.Exp).then_inc(q["em_ready"], 1)
                if i == 4:
                    act.wait_ge(q["u_done"], u + 1)
                    wait(act, q["gin_ps"], u)
                    fn(xcT[:, :], u1[:, :], ACT.Relu, bias=bnb[:, 1:2]).then_inc(q["xc_ready"], 1)
                    act.wait_ge(q["nmp_ps"], u + 1)
                    fn(nmT[:, :], B[:, 0, :], ACT.Copy).then_inc(q["nmT_ready"], 1)
                if i == 5:
                    act.wait_ge(q["r_ps"], u + 1)
                    wait(act, q["rr_done"], u)
                    fn(tr[:, :], B[:, 2, :], ACT.Tanh, bias=gb[:, 0:1], scale=0.5).then_inc(q["tr_ready"], 1)
                    act.wait_ge(q["z_ps"], u + 1)
                    wait(act, q["zd_done"], u)
                    fn(tz[:, :], B[:, 1, :], ACT.Tanh, bias=gb[:, 1:2], scale=0.5).then_inc(q["tz_ready"], 1)
                if i == 6:
                    act.wait_ge(q["g2_done"], u + 1)
                    wait(act, q["dx_done"], u)
                    fn(nT[:, :], g2[:, :], ACT.Tanh, bias=col[:, C_BIN:C_BIN + 1]).then_inc(q["n_ready"], 1)
                if i == 8:
                    act.wait_ge(q["x2t_ps"], u + 1)
                    wait(act, q["h2_ps"], u)
                    fn(x2T[:, :], B[:, 0, :], ACT.Copy).then_inc(q["x2T_ready"], 1)
                    act.wait_ge(q["hb_done"], u + 1)
                    wait(act, q["wr_done"], u)
                    fn(eg[:, :, :], h2[:, :, N:HC], ACT.Exp).then_inc(q["eg_ready"], 1)
                if i == 11:
                    act.wait_ge(q["x3t_ps"], u + 1)
                    wait(act, q["e3_ps"], H3 * u)
                    fn(x3T[:, :], B[:, 2, :], ACT.Copy).then_inc(q["x3T_ready"], 1)
                    act.wait_ge(q["h3_ps"], u + 1)
                    wait(act, q["pv3_ps"], H3 * u)
                    fn(h3[:, :, :].rearrange("p (a b) c -> p a (b c)", a=2), B[:, 0:2, 0:2 * GC], ACT.Copy)\
                        .then_inc(q["h3_ready"], 1)
                    act.wait_ge(q["h3_ready"], u + 1)
                if 11 <= i < 11 + H3:
                    h = i - 11
                    act.wait_ge(q["e3_ps"], H3 * u + h + 1)
                    wait(act, q["l3_done"], H3 * u + h - 1)
                    for b in range(GB):
                        last = fn(g(z3[:, h % 2, :], b), g(B[:, 2, :], b), ACT.Identity,
                                  bias=h3[:, b, N + h:N + h + 1])
                    last.then_inc(q["z3_ready"], 1)
                    act.wait_ge(q["nm3_ready"], H3 * u + h + 1)
                    wait(act, q["p3_ready"], H3 * u + h - 1)
                    for b in range(GB):
                        last = fn(g(e3[:, h % 2, :], b), g(l3[:, h % 2, :], b), ACT.Exp,
                                  bias=nm3[:, h % 2, b:b + 1], accum_out=sum3[:, h % 2, b:b + 1])
                    last.then_inc(q["exp3_done"], 1)
                if 12 <= i < 12 + H3:
                    h = i - 12
                    act.wait_ge(q["tr3_ps"], H3 * u + h + 1)
                    wait(act, q["pv3_ps"], H3 * u + h - 1)
                    fn(pT3[:, h % 2, :], B[:, 1, :], ACT.Copy).then_inc(q["pT3_ready"], 1)
                if i == 12 + H3:
                    act.wait_ge(q["pv3_ps"], H3 * u + H3)
                    wait(act, q["o3n_ps"], u)
                    fn(o3T[:, :], B[:, 0, :], ACT.Copy).then_inc(q["o3T_ready"], 1)

            act.wait_ge(q["prep"], 1)

            def step(k, p, front, back):
                s = 2 * k + p
                u = s - 1
                for i in range(SLOTS):
                    if front:
                        if i == 0:
                            project(s, p, k)
                        if 0 <= i - 1 < H0:
                            exps(s, i - 1)
                    if back:
                        back_slot(u, i)
                    if front:
                        if 0 <= i - 2 < H0:
                            probs_T(s, i - 2)
                        if i == H0 + 2:
                            act.wait_ge(q["pv_ps"], 8 * s + 8)
                            wait(act, q["wo_ps"], s)
                            fn(oT[:, :], O[:, :], ACT.Copy).then_inc(q["oT_ready"], 1)

            steps(act, step)

        @block.vector
        def _(dve):
            v = nc.vector
            dve.wait_ge(q["bn2_"], 1)
            v.tensor_tensor(bns[:, 0:1], bns[:, 0:1], col[:, C_G1:C_G1 + 1], ALU.mult)
            v.tensor_tensor(bns[:, 1:2], bns[:, 1:2], col[:, C_G2:C_G2 + 1], ALU.mult).then_inc(q["bn3_"], 1)
            dve.wait_ge(q["bn3_"], 1)
            v.tensor_tensor(bnt[:, 0:1], bns[:, 0:1], col[:, C_M1:C_M1 + 1], ALU.mult)
            v.tensor_tensor(bnt[:, 1:2], bns[:, 1:2], col[:, C_M2:C_M2 + 1], ALU.mult).then_inc(q["bn3_"], 1)
            v.tensor_tensor(gb[:, :], col[:, C_BIR:C_BIZ + 1], col[:, C_BHR:C_BHZ + 1], ALU.add)\
                .then_inc(q["bn4_"], 1)
            dve.wait_ge(q["bn3_"], 2)
            v.tensor_tensor(bnb[:, 0:1], col[:, C_B1:C_B1 + 1], bnt[:, 0:1], ALU.subtract)
            v.tensor_tensor(bnb[:, 1:2], col[:, C_B2:C_B2 + 1], bnt[:, 1:2], ALU.subtract)
            dve.wait_ge(q["bn4_"], 1)
            v.tensor_scalar(gb[:, :], gb[:, :], 0.5, None, ALU.mult)
            dve.wait_ge(q["rows_ps"], 1)
            v.tensor_copy(rowb[:, 0:H0 + 2 * N], B[:, 0, 0:H0 + 2 * N])
            dve.wait_ge(q["brow_ps"], 1)
            v.tensor_copy(brow[:, :], B[0:1, 1, 0:2]).then_inc(q["bn4_"], 1)
            dve.wait_ge(q["bn4_"], 2)
            v.tensor_tensor(brow[:, 0:1], brow[:, 0:1], row[:, R_AB:R_AB + 1], ALU.add).then_inc(q["brow_set"], 1)
            dve.wait_ge(q["wa_ps"], 1)
            v.tensor_copy(l2w[:, 0:N], wm[:, WL2:WL2 + N])
            v.tensor_copy(l2w[:, N:HC], B[:, 2, 0:2])
            v.tensor_copy(l3w[:, 0:N], wm[:, WL3:WL3 + N])
            v.tensor_copy(l3w[:, N:GC], S[0][:, 0:H3])
            v.tensor_copy(wa2[:, :], S[0][:, H3:2 * H3]).then_inc(q["wa_set"], 1)
            dve.wait_ge(q["wa_set"], 1)
            for h in range(H3):
                v.tensor_scalar(wa2b[:, h, :], ones[:, :], wa2[:, h:h + 1], None, ALU.mult)
            dve.wait_ge(q["bl2_ps"], 1)
            dve.wait_ge(q["const_set"], 4)
            v.tensor_copy(rowb[:, H0 + 2 * N:H0 + 2 * N + 2], S[1][:, 0:2]).then_inc(q["prep"], 1)
            dve.wait_ge(q["prep"], 1)

            def layer_norm(i, u, src, dst, free):
                for b in range(GB):
                    last = v.bn_stats(stats[i][:, b, :], g(src, b))
                last.then_inc(ln_stats[i], 1)
                dve.wait_ge(q["prep"], 1)
                dve.wait_ge(ln_stats[i], u + 1)
                for b in range(GB):
                    last = v.bn_aggr(meanv[i][:, b, :], stats[i][:, b, :])
                last.then_inc(ln_aggr[i], 1)

            def layer_norm_end(i, u, src, dst):
                dve.wait_ge(ln_rstd[i], u + 1)
                dve.wait_ge(ln_aggr[i], u + 1)
                for b in range(GB):
                    last = v.tensor_scalar(g(dst, b), g(src, b), meanv[i][:, b, 0:1], rstd[i][:, b:b + 1],
                                           ALU.subtract, ALU.mult)
                last.then_inc(ln_out[i], 1)

            def masks(s, p, k):
                dve.wait_ge(loaded[p], (k + 1) * 4 * DMA)
                wait(dve, q["qk_ps"], 8 * s)
                v.tensor_scalar(mask0[:, :], an[p][:, :], 0.0, NEG0, ALU.is_equal, ALU.mult)\
                    .then_inc(q["mask0_ready"], 1)
                wait(dve, q["e3_ps"], H3 * (s - 1))
                v.tensor_scalar(mask3[p][:, :], an[p][:, :], 0.0, NEG3, ALU.is_le, ALU.mult)\
                    .then_inc(q["mask3_ready"], 1)

            def scores(s, h, p):
                dve.wait_ge(q["qk_ps"], 8 * s + h + 1)
                wait(dve, q["exp_done"], 8 * s + h - 1)
                v.scalar_tensor_tensor(out=sc0[:, h % 2, :], in0=an[p][:, :], scalar=we[:, h:h + 1],
                                       in1=S[h % 2][:, :], op0=ALU.mult, op1=ALU.add).then_inc(q["sc_ready"], 1)
                dve.wait_ge(q["sc_ready"], 8 * s + h + 1)
                v.tensor_reduce(nm0[:, h % 2, :], per(sc0[:, h % 2, :]), AX, ALU.max, negate=True)\
                    .then_inc(q["nm_ready"], 1)

            def norm(s, h):
                dve.wait_ge(q["exp_done"], 8 * s + h + 1)
                v.reciprocal(rec0[:, h % 2, :], sum0[:, h % 2, :]).then_inc(q["rec_done"], 1)
                dve.wait_ge(q["rec_done"], 8 * s + h + 1)
                wait(dve, q["tr_ps"], 8 * s + h - 1)
                v.tensor_tensor(per(p0[:, h % 2, :]), per(e0[:, h % 2, :]), wide(rec0[:, h % 2, :]), ALU.mult)\
                    .then_inc(q["p_ready"], 1)

            def front_end(s, p):
                dve.wait_ge(q["wo_ps"], s + 1)
                wait(dve, ln_out[0], s)
                v.tensor_tensor(r0[:, :], J[:, :], xn[p][:, :], ALU.add).then_inc(q["res0_done"], 1)
                dve.wait_ge(q["res0_done"], s + 1)
                layer_norm(0, s, r0, x1, None)

            def back_slot(u, i):
                if i == 1:
                    dve.wait_ge(q["sq_ready"], u + 1)
                    dve.wait_ge(q["dd_ready"], u + 1)
                    wait(dve, q["arg_ps"], u)
                    v.scalar_tensor_tensor(out=lr[:, :], in0=dd[:, :], scalar=sel[:, 0:1], in1=sqr[:, :],
                                           op0=ALU.mult, op1=ALU.subtract)
                    v.scalar_tensor_tensor(out=ll[:, :], in0=dd[:, :], scalar=sel2[:, 0:1], in1=sql[:, :],
                                           op0=ALU.mult, op1=ALU.add).then_inc(q["lr_done"], 1)
                    dve.wait_ge(q["msg_ps"], u + 1)
                    wait(dve, q["msg_ready"], u)
                    v.tensor_tensor(per(m1[:, :]), per(B[:, 0, :]),
                                    bmsg.unsqueeze(1).broadcast_to([128, GB, N]), ALU.add)\
                        .then_inc(q["m1_done"], 1)
                if i == 4:
                    dve.wait_ge(q["c2_ps"], u + 1)
                    dve.wait_ge(q["x1T_ready"], u + 1)
                    wait(dve, q["xc_ready"], u)
                    v.scalar_tensor_tensor(out=u1[:, :], in0=B[:, 1, :], scalar=bns[:, 1:2], in1=x1T[:, :],
                                           op0=ALU.mult, op1=ALU.add).then_inc(q["u_done"], 1)
                if i == 5:
                    dve.wait_ge(q["tr_ready"], u + 1)
                    v.tensor_scalar(rr[:, :], tr[:, :], 0.5, 0.5, ALU.mult, ALU.add).then_inc(q["rr_done"], 1)
                    dve.wait_ge(q["rr_done"], u + 1)
                    dve.wait_ge(q["ghn_ps"], u + 1)
                    v.scalar_tensor_tensor(out=g1[:, :], in0=B[:, 0, :], scalar=col[:, C_BHN:C_BHN + 1],
                                           in1=rr[:, :], op0=ALU.add, op1=ALU.mult).then_inc(q["g1_done"], 1)
                    dve.wait_ge(q["g1_done"], u + 1)
                    dve.wait_ge(q["gin_ps"], u + 1)
                    wait(dve, q["n_ready"], u)
                    v.tensor_tensor(g2[:, :], B[:, 2, :], g1[:, :], ALU.add).then_inc(q["g2_done"], 1)
                if i == 7:
                    dve.wait_ge(q["dx_done"], u + 1)
                    dve.wait_ge(q["tz_ready"], u + 1)
                    v.scalar_tensor_tensor(out=zd[:, :], in0=tz[:, :], scalar=1.0, in1=dx[:, :],
                                           op0=ALU.add, op1=ALU.mult).then_inc(q["zd_done"], 1)
                    dve.wait_ge(q["zd_done"], u + 1)
                    wait(dve, q["yt_ps"], u)
                    v.scalar_tensor_tensor(out=yT[:, :], in0=zd[:, :], scalar=0.5, in1=nx[:, :],
                                           op0=ALU.mult, op1=ALU.add).then_inc(q["y_done"], 1)
                    dve.wait_ge(q["yt_ps"], u + 1)
                    layer_norm(1, u, B[:, 1, :], x2, None)
                    wait(dve, q["x2t_ps"], u)
                    wait(dve, q["r2_done"], u)
                    layer_norm_end(1, u, B[:, 1, :], x2)
                if i == 8:
                    dve.wait_ge(q["h2_ps"], u + 1)
                    wait(dve, q["hg_done"], u)
                    for a in range(2):
                        last = v.tensor_tensor(h2[:, 2 * a:2 * a + 2, :],
                                               B[:, 1 + a, 0:2 * HC].rearrange("p (b c) -> p b c", c=HC),
                                               bl2.unsqueeze(1).broadcast_to([128, 2, HC]), ALU.add)
                    last.then_inc(q["hb_done"], 1)
                    dve.wait_ge(q["hb_done"], u + 1)
                    dve.wait_ge(q["eg_ready"], u + 1)
                    wait(dve, q["num_ps"], u)
                    v.tensor_tensor(hg[:, :, 0:N], h2[:, :, 0:N], wide(eg[:, :, 1]), ALU.mult)
                    v.tensor_copy(hg[:, :, N:HC], eg[:, :, 1:2].broadcast_to([128, GB, 2])).then_inc(q["hg_done"], 1)
                if i == 9:
                    num = B[:, 0:2, 0:2 * HC].rearrange("p a (b c) -> p a b c", c=HC)
                    dve.wait_ge(q["num_ps"], u + 1)
                    v.tensor_tensor(dn[:, :].rearrange("p (a b) -> p a b", a=2), num[:, :, :, N],
                                    eg[:, :, 0].rearrange("p (a b) -> p a b", a=2), ALU.mult)\
                        .then_inc(q["dn_done"], 1)
                    dve.wait_ge(q["dn_done"], u + 1)
                    v.reciprocal(rdn[:, :], dn[:, :]).then_inc(q["rdn_done"], 1)
                    dve.wait_ge(q["rdn_done"], u + 1)
                    v.tensor_tensor(wr[:, :], rdn[:, :], eg[:, :, 0], ALU.mult).then_inc(q["wr_done"], 1)
                    dve.wait_ge(q["wr_done"], u + 1)
                    dve.wait_ge(ln_out[1], u + 1)
                    wait(dve, ln_out[2], u)
                    for b in range(GB):
                        last = v.scalar_tensor_tensor(out=g(r2, b), in0=num[:, b // 2, b % 2, 0:N],
                                                      scalar=wr[:, b:b + 1], in1=g(x2, b),
                                                      op0=ALU.mult, op1=ALU.add)
                    last.then_inc(q["r2_done"], 1)
                    dve.wait_ge(q["r2_done"], u + 1)
                    layer_norm(2, u, r2, x3, None)
                if i == 10:
                    wait(dve, q["x3t_ps"], u)
                    wait(dve, q["r3_done"], u)
                    layer_norm_end(2, u, r2, x3)
                if 11 <= i < 11 + H3:
                    h = i - 11
                    dve.wait_ge(q["z3_ready"], H3 * u + h + 1)
                    wait(dve, q["exp3_done"], H3 * u + h - 1)
                    v.scalar_tensor_tensor(out=l3[:, h % 2, :], in0=z3[:, h % 2, :], scalar=SLOPE,
                                           in1=z3[:, h % 2, :], op0=ALU.mult, op1=ALU.max)\
                        .then_inc(q["l3_done"], 1)
                    dve.wait_ge(q["l3_done"], H3 * u + h + 1)
                    v.tensor_reduce(nm3[:, h % 2, :], per(l3[:, h % 2, :]), AX, ALU.max, negate=True)\
                        .then_inc(q["nm3_ready"], 1)
                    dve.wait_ge(q["exp3_done"], H3 * u + h + 1)
                    v.reciprocal(rec3[:, h % 2, :], sum3[:, h % 2, :]).then_inc(q["rec3_done"], 1)
                    dve.wait_ge(q["rec3_done"], H3 * u + h + 1)
                    wait(dve, q["tr3_ps"], H3 * u + h - 1)
                    v.tensor_tensor(per(p3[:, h % 2, :]), per(e3[:, h % 2, :]), wide(rec3[:, h % 2, :]),
                                    ALU.mult).then_inc(q["p3_ready"], 1)
                if i == 12 + H3:
                    dve.wait_ge(q["o3n_ps"], u + 1)
                    dve.wait_ge(ln_out[2], u + 1)
                    wait(dve, ln_out[3], u)
                    v.tensor_tensor(r3[:, :], B[:, 1, :], x3[:, :], ALU.add).then_inc(q["r3_done"], 1)
                    dve.wait_ge(q["r3_done"], u + 1)
                    layer_norm(3, u, r3, None, None)

            def step(k, p, front, back):
                s = 2 * k + p
                u = s - 1
                for i in range(SLOTS):
                    if front:
                        if i == 0:
                            masks(s, p, k)
                        if 0 <= i - 1 < H0:
                            scores(s, i - 1, p)
                        if 0 <= i - 2 < H0:
                            norm(s, i - 2)
                    if back:
                        back_slot(u, i)
                    if front:
                        if i == H0 + 3:
                            front_end(s, p)
                        if i == H0 + 4:
                            wait(dve, q["x1t_ps"], s)
                            layer_norm_end(0, s, r0, x1)
                    if back and i == 12 + H3:
                        wait(dve, stored[1 - p], (k + p - 1) * DMA)
                        layer_norm_end(3, u, r3, xo[1 - p])

            steps(dve, step)


SLOTS = 13 + H3


def kernel(**inputs):
    import numpy as np
    import concourse.bacc as bacc
    from concourse.bass_utils import run_bass_kernel_spmd

    i = {n: np.ascontiguousarray(a) for n, a in inputs.items()}
    flat = lambda a: np.ascontiguousarray(a.reshape(N, -1))
    wih = i["L1_gnn_w_ih"].T
    mats = np.concatenate(
        [i["L0_gnn_W_q"].T, i["L0_gnn_W_k"].T, i["L0_gnn_W_v"].T, i["L0_gnn_W_o"].T,
         i["L1_gnn_conv1_w"][:, :, 0].T, i["L1_gnn_w_msg"].T, i["L2_gnn_W_w"].T, i["L2_gnn_W_w"],
         i["L3_gnn_W"], i["L3_gnn_W"].T, i["L1_gnn_w_hh"].T, wih[0:N], wih[N:2 * N],
         i["L1_gnn_conv2_w"].transpose(1, 2, 0).reshape(N, TAPS * N)], axis=1)
    bih, bhh = i["L1_gnn_b_ih"], i["L1_gnn_b_hh"]
    cols = np.stack(
        [i["L1_gnn_bn1_g"], i["L1_gnn_bn1_b"], i["L1_gnn_bn1_m"], i["L1_gnn_bn1_v"],
         i["L1_gnn_bn2_g"], i["L1_gnn_bn2_b"], i["L1_gnn_bn2_m"], i["L1_gnn_bn2_v"],
         bih[0:N], bih[N:2 * N], bih[2 * N:], bhh[0:N], bhh[N:2 * N], bhh[2 * N:],
         i["L2_gnn_a_w"][0:N], i["L2_gnn_a_w"][N:], i["L2_gnn_W_b"]], axis=1)
    rows = np.concatenate([i["L0_gnn_W_e"][:, 0], i["L1_gnn_b_msg"], i["L2_gnn_W_b"], i["L2_gnn_a_b"]])[None, :]
    arrays = {
        "x_n": flat(i["x"].transpose(1, 0, 2)), "x_t": flat(i["x"].transpose(2, 0, 1)),
        "adj_n": flat(i["adj"].transpose(1, 0, 2)), "adj_t": flat(i["adj"].transpose(2, 0, 1)),
        "mats": np.ascontiguousarray(mats),
        "wse": np.ascontiguousarray(np.concatenate([i["L1_gnn_w_se"].T] * 3, axis=1)),
        "cols": np.ascontiguousarray(cols), "rows": np.ascontiguousarray(rows),
        "bse": np.ascontiguousarray(np.concatenate([i["L1_gnn_b_se"]] * 3)[:, None]),
        "att3": i["L3_gnn_a"],
    }
    nc = bacc.Bacc("TRN2", target_bir_lowering=False, num_devices=1)
    args = [nc.dram_tensor(f"in_{n}", a.shape, F32, kind="ExternalInput").ap() for n, a in arrays.items()]
    out = nc.dram_tensor("out_x", (N, N * N), F32, kind="ExternalOutput").ap()
    build(nc, *args, out)
    r = run_bass_kernel_spmd(nc, [{f"in_{n}": a for n, a in arrays.items()}], core_ids=[0])
    return np.ascontiguousarray(r.results[0]["out_x"].reshape(N, N, N).transpose(1, 0, 2))
```

```python
from contextlib import ExitStack

import concourse.bass as bass
from concourse import mybir

F32 = mybir.dt.float32
BF16 = mybir.dt.bfloat16
ALU = mybir.AluOpType
ACT = mybir.ActivationFunctionType
AX = mybir.AxisListType.X

N = 128
GB = 4
W = GB * N
GROUPS = N // GB
H0, D0 = 8, 16
H3, D3 = 4, 32
TAPS, PAD = 17, 8
Q = N // 4
QP = Q + PAD // 2
EPS = 1e-5
NEG0 = -1.0e30
NEG3 = -9.0e15
SLOPE = 0.2
NS = 3
KS = 3 * NS
HC = N + 2
GC = N + H3
DMA = 16

(C_G1, C_B1, C_M1, C_V1, C_G2, C_B2, C_M2, C_V2, C_BIR, C_BIZ, C_BIN, C_BHR, C_BHZ, C_BHN, C_A1, C_A2,
 C_WB) = range(17)
NCOL = 17
R_WE, R_BM, R_WB, R_AB = 0, H0, H0 + N, H0 + 2 * N
NROW = H0 + 2 * N + 1
WQ, WK, WV, WO, W1, WM, WL2, WL2N, WL3, WL3T, WHH = (N * i for i in range(11))
WIC, WIN, WC2 = N * 13, N * 16, N * 19
NMAT = N * (19 + TAPS)


def build(nc, x_n, x_t, adj_n, adj_t, mats, wse, cols, rows, bse, att3, out):
    with ExitStack() as ctx:
        def sb(name, shape, dt=F32):
            return ctx.enter_context(nc.sbuf_tensor(name, shape, dt))

        def ps(name, shape, dt=F32):
            return ctx.enter_context(nc.psum_tensor(name, shape, dt))

        def sem(name):
            return ctx.enter_context(nc.semaphore(name))

        wm = sb("wm", [128, NMAT])
        col = sb("col", [128, NCOL])
        row = sb("row", [1, NROW])
        wse_s = sb("wse_s", [128, KS])
        bse_s = sb("bse_s", [KS, 1])
        att = sb("att", [128, 2 * H3])
        ident = sb("ident", [128, 128])
        identb = sb("identb", [128, 128], BF16)
        ones = sb("ones", [128, 128])
        headm = sb("headm", [128, H0])
        sel = sb("sel", [KS, 4])
        sel2 = sb("sel2", [KS, 1])
        neghalf = sb("neghalf", [128, GB])
        eps4 = sb("eps4", [128, GB])
        bns = sb("bns", [128, 2])
        bnt = sb("bnt", [128, 2])
        bnb = sb("bnb", [128, 2])
        gb = sb("gb", [128, 2])
        rowb = sb("rowb", [128, H0 + 2 * N + 2])
        brow = sb("brow", [1, 2])
        l2w = sb("l2w", [128, HC])
        l3w = sb("l3w", [128, GC])
        wa2 = sb("wa2", [128, H3])
        wa2b = sb("wa2b", [128, H3, 128])
        we = rowb[:, 0:H0]
        bmsg = rowb[:, H0:H0 + N]
        bl2 = rowb[:, H0 + N:H0 + 2 * N + 2]

        xn = [sb(f"xn{p}", [128, W]) for p in range(2)]
        xt = [sb(f"xt{p}", [128, W]) for p in range(2)]
        an = [sb(f"an{p}", [128, W]) for p in range(2)]
        at = [sb(f"at{p}", [128, W]) for p in range(2)]
        mask3 = [sb(f"mask3{p}", [128, W], BF16) for p in range(2)]
        mask0 = sb("mask0", [128, W], BF16)
        qT = sb("qT", [128, W])
        kT = sb("kT", [128, W])
        kh = sb("kh", [128, H0, W])
        vpad = sb("vpad", [128, GB * H0 * 32])
        sc0 = sb("sc0", [128, 2, W])
        nm0 = sb("nm0", [128, 2, GB])
        e0 = sb("e0", [128, 2, W])
        sum0 = sb("sum0", [128, 2, GB])
        rec0 = sb("rec0", [128, 2, GB])
        p0 = sb("p0", [128, 2, W])
        pT0 = sb("pT0", [128, 2, W])
        oT = sb("oT", [128, W])
        r0 = sb("r0", [128, W])
        x1 = sb("x1", [128, W])
        x1T = sb("x1T", [128, W])
        xs = sb("xs", [128, 8, GB, QP])
        xd = sb("xd", [128, 3, GB, QP])
        xf = sb("xf", [128, 3, GB, QP])
        wsum = sb("wsum", [128, 5, 4, N])
        vT = sb("vT", [128, W])
        dd = sb("dd", [KS, W])
        sql = sb("sql", [KS, W])
        sqr = sb("sqr", [KS, W])
        ll = sb("ll", [KS, W])
        lr = sb("lr", [KS, W])
        m1 = sb("m1", [128, W])
        msg = sb("msg", [128, W])
        em = sb("em", [128, W])
        aT = sb("aT", [128, W])
        u1 = sb("u1", [128, W])
        xcT = sb("xcT", [128, W])
        nmT = sb("nmT", [128, W])
        tr = sb("tr", [128, W])
        tz = sb("tz", [128, W])
        rr = sb("rr", [128, W])
        g1 = sb("g1", [128, W])
        g2 = sb("g2", [128, W])
        nT = sb("nT", [128, W])
        dx = sb("dx", [128, W])
        nx = sb("nx", [128, W])
        zd = sb("zd", [128, W])
        yT = sb("yT", [128, W])
        x2 = sb("x2", [128, W])
        x2T = sb("x2T", [128, W])
        h2 = sb("h2", [128, GB, HC])
        eg = sb("eg", [128, GB, 2])
        hg = sb("hg", [128, GB, HC])
        dn = sb("dn", [128, GB])
        rdn = sb("rdn", [128, GB])
        wr = sb("wr", [128, GB])
        r2 = sb("r2", [128, W])
        x3 = sb("x3", [128, W])
        x3T = sb("x3T", [128, W])
        h3 = sb("h3", [128, GB, GC])
        z3 = sb("z3", [128, 2, W])
        l3 = sb("l3", [128, 2, W])
        nm3 = sb("nm3", [128, 2, GB])
        e3 = sb("e3", [128, 2, W])
        sum3 = sb("sum3", [128, 2, GB])
        rec3 = sb("rec3", [128, 2, GB])
        p3 = sb("p3", [128, 2, W])
        pT3 = sb("pT3", [128, 2, W])
        o3T = sb("o3T", [128, W])
        r3 = sb("r3", [128, W])
        xo = [sb(f"xo{p}", [128, W]) for p in range(2)]
        stats = [sb(f"stats{i}", [128, GB, 6]) for i in range(4)]
        meanv = [sb(f"meanv{i}", [128, GB, 2]) for i in range(4)]
        veps = [sb(f"veps{i}", [128, GB]) for i in range(4)]
        rstd = [sb(f"rstd{i}", [128, GB]) for i in range(4)]

        S = [ps("S0", [128, W]), ps("S1", [128, W])]
        T = ps("T", [128, W])
        O = ps("O", [128, W])
        M = ps("M", [128, 2, W])
        L = ps("L", [128, 2, W])

        names = """wload wcol ones_set pads_set sel_set id_set const_set bn1_ bn2_ bn3_ bn4_ rows_ps rowb_set
            brow_ps brow_set bl2_ps bl2_set wa_ps wa_set wa2b_set prep
            q_ps k_ps v_ps qT_ready kT_ready v_ready mask0_ready mask3_ready oT_ready wo_ps res0_done
            x1t_ps x1T_ready c1_ps hp_ready x1_ready x2_ready wsum_set cp_ps v1_done v2_done d_ps dd_ready sq_ready lr_done msg_ps m1_done msg_ready c2_ps
            u_done xc_ready arg_ps em_ready aT_done nmp_ps nmT_ready ghn_ps r_ps tr_ready z_ps tz_ready
            gin_ps rr_done g1_done g2_done n_ready dx_done zd_done y_done yt_ps
            x2t_ps x2T_ready h2_ps hb_done eg_ready hg_done num_ps dn_done rdn_done wr_done r2_done
            x3t_ps x3T_ready h3_ps h3_ready o3T_ready o3n_ps r3_done""".split()
        per_head = """kh_ready qk_ps sc_ready nm_ready exp_done rec_done p_ready tr_ps pT_ready pv_ps
            e3_ps z3_ready l3_done nm3_ready exp3_done rec3_done p3_ready tr3_ps pT3_ready pv3_ps""".split()
        q = {n: sem(n) for n in names + per_head}
        loaded = [sem("loaded0"), sem("loaded1")]
        loaded_t = [sem("loaded_t0"), sem("loaded_t1")]
        stored = [sem("stored0"), sem("stored1")]
        ln_stats = [sem(f"ln_stats{i}") for i in range(4)]
        ln_aggr = [sem(f"ln_aggr{i}") for i in range(4)]
        ln_veps = [sem(f"ln_veps{i}") for i in range(4)]
        ln_rstd = [sem(f"ln_rstd{i}") for i in range(4)]
        ln_out = [sem(f"ln_out{i}") for i in range(4)]

        def g(t, b):
            return t[:, b * N:(b + 1) * N]

        def per(t):
            return t.rearrange("p (b n) -> p b n", b=GB)

        def phases(t):
            return t.rearrange("p (b c r) -> p c b r", b=GB, c=4)

        def wide(s):
            return s.unsqueeze(2).broadcast_to([128, GB, N])

        def wait(eng, s, value):
            if isinstance(value, int) and value <= 0:
                return
            eng.wait_ge(s, value)

        def steps(eng, step):
            step(0, 0, True, False, False)
            step(0, 1, True, True, False)
            step(1, 0, True, True, True)
            step(1, 1, True, True, True)
            with eng.Fori(2, GROUPS // 2) as k:
                step(k, 0, True, True, True)
                step(k, 1, True, True, True)
            step(GROUPS // 2, 0, False, True, True)
            step(GROUPS // 2, 1, False, False, True)

        block = ctx.enter_context(nc.Block())

        @block.sync
        def _(sp):
            def load(t, p):
                for dst, src in ((xt, x_t), (an, adj_n), (xn, x_n)):
                    sp.dma_start(dst[p][:, :], src[:, bass.ds(t * W, W)]).then_inc(loaded[p], DMA)

            def load_t(t, p):
                sp.dma_start(at[p][:, :], adj_t[:, bass.ds(t * W, W)]).then_inc(loaded_t[p], DMA)

            def load_t_next(t, p):
                sp.wait_ge(q["num_ps"], t - 1)
                load_t(t, p)

            def load_next(t, p):
                sp.wait_ge(q["v_ps"], t + 1)
                sp.wait_ge(q["res0_done"], t + 1)
                sp.wait_ge(q["mask3_ready"], t + 1)
                load(t + 2, p)

            def store(t, p):
                sp.wait_ge(ln_out[3], t + 1)
                sp.dma_start(out[:, bass.ds(t * W, W)], xo[p][:, :]).then_inc(stored[p], DMA)

            sp.dma_start(wm[:, 0:WIC], mats[:, 0:WIC]).then_inc(q["wload"], DMA)
            load(0, 0)
            sp.dma_start(col[:, :], cols).then_inc(q["wcol"], DMA)
            sp.dma_start(row[:, :], rows).then_inc(q["wcol"], DMA)
            sp.dma_start(wse_s[:, :], wse).then_inc(q["wcol"], DMA)
            sp.dma_start(bse_s[:, :], bse).then_inc(q["wcol"], DMA)
            sp.wait_ge(q["pads_set"], 1)
            for h in range(H3):
                for j in range(2):
                    sp.dma_start(att[h * D3:(h + 1) * D3, j * H3 + h:j * H3 + h + 1],
                                 att3[h, j * D3:(j + 1) * D3].rearrange("(d o) -> d o", o=1))\
                        .then_inc(q["wcol"], DMA)
            sp.dma_start(wm[:, WIC:NMAT], mats[:, WIC:NMAT]).then_inc(q["wload"], DMA)
            load(1, 1)
            load_t(0, 0)
            load_t(1, 1)
            load_next(0, 0)
            load_next(1, 1)
            with sp.Fori(1, GROUPS // 2 - 1) as k:
                for p in range(2):
                    load_t_next(2 * k + p, p)
                    load_next(2 * k + p, p)
                    store(2 * k + p - 2, p)
            for t in (GROUPS - 2, GROUPS - 1):
                load_t_next(t, t % 2)
                store(t - 2, t % 2)
            store(GROUPS - 2, 0)
            store(GROUPS - 1, 1)
            sp.wait_ge(stored[0], DMA * GROUPS // 2)
            sp.wait_ge(stored[1], DMA * GROUPS // 2)

        @block.gpsimd
        def _(pool):
            pool.memset(ones[:, :], 1.0).then_inc(q["ones_set"], 1)
            pool.memset(att[:, :], 0.0)
            pool.memset(xs[:, :, :, :], 0.0)
            pool.memset(neghalf[:, :], -0.5)
            pool.memset(eps4[:, :], EPS)
            pool.memset(vpad[:, :], 0.0).then_inc(q["pads_set"], 1)
            pool.memset(sel[:, :], 1.0)
            pool.memset(ident[:, :], 0.0).then_inc(q["sel_set"], 1)
            pool.memset(headm[:, :], 1.0).then_inc(q["sel_set"], 1)
            pool.wait_ge(q["sel_set"], 2)
            pool.affine_select(out=ident[:, :], in_=ident[:, :], compare_op=ALU.not_equal, fill=1.0, base=0,
                               pattern=[[-1, 128]], channel_multiplier=1).then_inc(q["id_set"], 1)
            pool.affine_select(out=headm[:, :], in_=headm[:, :], compare_op=ALU.is_ge, fill=0.0, base=0,
                               pattern=[[-D0, H0]], channel_multiplier=1).then_inc(q["id_set"], 1)
            pool.affine_select(out=sel[:, :], in_=sel[:, :], compare_op=ALU.is_ge, fill=0.0, base=0,
                               pattern=[[-NS, 4]], channel_multiplier=1).then_inc(q["id_set"], 1)
            pool.wait_ge(q["id_set"], 3)
            pool.affine_select(out=headm[:, :], in_=headm[:, :], compare_op=ALU.is_ge, fill=0.0, base=D0 - 1,
                               pattern=[[D0, H0]], channel_multiplier=-1).then_inc(q["const_set"], 1)
            pool.affine_select(out=sel[:, :], in_=sel[:, :], compare_op=ALU.is_ge, fill=0.0, base=NS - 1,
                               pattern=[[NS, 4]], channel_multiplier=-1).then_inc(q["const_set"], 1)
            pool.tensor_copy(identb[:, :], ident[:, :]).then_inc(q["const_set"], 1)
            pool.wait_ge(q["const_set"], 2)
            pool.tensor_scalar(sel2[:, :], sel[:, 0:1], 2.0, 1.0, ALU.mult, ALU.mult).then_inc(q["const_set"], 1)
            pool.wait_ge(q["wcol"], 12 * DMA)
            pool.wait_ge(q["const_set"], 4)
            for j, v in enumerate((C_V1, C_V2)):
                pool.tensor_scalar(bnt[:, j:j + 1], col[:, v:v + 1], EPS, 1.0, ALU.add, ALU.mult)\
                    .then_inc(q["bn1_"], 1)
            pool.wait_ge(q["bn1_"], 2)
            pool.tensor_tensor(bns[:, :], bnt[:, :], neghalf[:, 0:2], ALU.pow).then_inc(q["bn2_"], 1)

            def rsqrt(i, u):
                pool.wait_ge(ln_aggr[i], u + 1)
                pool.tensor_tensor(veps[i][:, :], meanv[i][:, :, 1], eps4[:, :], ALU.add)\
                    .then_inc(ln_veps[i], 1)
                pool.wait_ge(ln_veps[i], u + 1)
                pool.tensor_tensor(rstd[i][:, :], veps[i][:, :], neghalf[:, :], ALU.pow)\
                    .then_inc(ln_rstd[i], 1)

            def k_heads(s):
                wait(pool, q["wo_ps"], s)
                pool.wait_ge(q["kT_ready"], s + 1)
                pool.tensor_tensor(kh[:, 0, :], kT[:, :], headm[:, 0:1].broadcast_to([128, W]), ALU.mult)\
                    .then_inc(q["kh_ready"], 1)
                for h in range(1, H0):
                    pool.tensor_scalar(kh[:, h, :], kT[:, :], headm[:, h:h + 1], 1.0, ALU.mult, ALU.mult)\
                        .then_inc(q["kh_ready"], 1)

            def step(k, p, l0, l1, l23):
                t = 2 * k + p
                m, u = t - 1, t - 2
                if l0:
                    k_heads(t)
                if l1:
                    pool.wait_ge(q["hp_ready"], m + 1)
                    wait(pool, q["c2_ps"], m)
                    e, o = xs[:, 6:8], xs[:, 4:6]
                    tt = pool.tensor_tensor
                    tt(xs[:, 0:2].rearrange("p y b i -> p (y b i)"), e.rearrange("p y b i -> p (y b i)"),
                       o.rearrange("p y b i -> p (y b i)"), ALU.subtract)
                    tt(xs[:, 2], e[:, 1], o[:, 0], ALU.subtract)
                    tt(xs[:, 3, :, 0:QP - 1], e[:, 0, :, 1:QP], o[:, 1, :, 0:QP - 1], ALU.subtract)\
                        .then_inc(q["x1_ready"], 1)
                    pool.wait_ge(q["x1_ready"], m + 1)
                    x2l = xs[:, 0:6].rearrange("p (k y) b i -> p k y b i", y=2)
                    tt(xd[:, :, :, :], x2l[:, :, 0], x2l[:, :, 1], ALU.subtract)
                    tt(xf[:, :, :, 0:QP - 1], x2l[:, :, 0, :, 1:QP], x2l[:, :, 1, :, 0:QP - 1], ALU.subtract)\
                        .then_inc(q["x2_ready"], 1)
                if l23:
                    rsqrt(2, u)
                if l1:
                    pool.wait_ge(loaded_t[1 - p], (k + p) * DMA)
                    pool.wait_ge(q["em_ready"], m + 1)
                    wait(pool, q["nmp_ps"], m)
                    pool.tensor_tensor(aT[:, :], em[:, :], at[1 - p][:, :], ALU.mult).then_inc(q["aT_done"], 1)
                if l1:
                    pool.wait_ge(q["n_ready"], m + 1)
                    wait(pool, q["y_done"], m)
                    pool.tensor_tensor(dx[:, :], x1T[:, :], nT[:, :], ALU.subtract)
                    pool.tensor_tensor(nx[:, :], x1T[:, :], nT[:, :], ALU.add).then_inc(q["dx_done"], 1)
                if l0:
                    rsqrt(0, t)
                if l1:
                    rsqrt(1, m)
                if l23:
                    rsqrt(3, u)

            steps(pool, step)

        @block.tensor
        def _(pe):
            mm = nc.tensor.matmul

            pe.wait_ge(q["ones_set"], 1)
            pe.wait_ge(q["wcol"], 12 * DMA)
            pe.wait_ge(q["wload"], 2 * DMA)
            mm(M[:, 0, 0:NROW - 1], ones[0:1, :], row[:, 0:NROW - 1], start=True, stop=True)\
                .then_inc(q["rows_ps"], 1)
            mm(M[0:1, 1, 0:2], col[:, C_WB:C_WB + 1], col[:, C_A1:C_A2 + 1], start=True, stop=True)\
                .then_inc(q["brow_ps"], 1)
            mm(L[:, 0, 0:2], wm[:, WL2N:WL2N + N], col[:, C_A1:C_A2 + 1], start=True, stop=True)
            mm(S[0][:, 0:2 * H3], wm[:, WL3T:WL3T + N], att[:, :], start=True, stop=True).then_inc(q["wa_ps"], 1)
            pe.wait_ge(q["brow_set"], 1)
            mm(S[1][:, 0:2], ones[0:1, :], brow[:, :], start=True, stop=True).then_inc(q["bl2_ps"], 1)
            pe.wait_ge(q["prep"], 1)

            def transpose4(dst, src):
                for b in range(GB):
                    last = nc.tensor.transpose(g(dst, b), g(src, b), ident[:, :])
                return last

            def project(s, p, k):
                pe.wait_ge(loaded[p], (k + 1) * 3 * DMA)
                wait(pe, q["sc_ready"], 8 * s)
                mm(S[0][:, :], wm[:, WQ:WQ + N], xt[p][:, :], start=True, stop=True).then_inc(q["q_ps"], 1)
                mm(S[1][:, :], wm[:, WK:WK + N], xt[p][:, :], start=True, stop=True).then_inc(q["k_ps"], 1)
                wait(pe, q["res0_done"], s)
                for b in range(GB):
                    last = mm(g(T, b), g(xt[p], b), wm[:, WV:WV + N], start=True, stop=True)
                last.then_inc(q["v_ps"], 1)

            def scores(s, h):
                if h == 0:
                    pe.wait_ge(q["mask0_ready"], s + 1)
                    pe.wait_ge(q["qT_ready"], s + 1)
                pe.wait_ge(q["kh_ready"], 8 * s + h + 1)
                wait(pe, q["sc_ready"], 8 * s + h - 1)
                mm(S[h % 2][:, :], identb[:, :], mask0[:, :], start=True, stop=False, skip_group_check=True)
                for b in range(GB):
                    last = mm(g(S[h % 2], b), g(qT, b), g(kh[:, h, :], b), start=False, stop=True,
                              skip_group_check=True)
                last.then_inc(q["qk_ps"], 1)

            def probs_T(s, h):
                pe.wait_ge(q["p_ready"], 8 * s + h + 1)
                wait(pe, q["pT_ready"], 8 * s + h)
                if h == 0:
                    pe.wait_ge(q["v_ready"], s + 1)
                transpose4(T, p0[:, h % 2, :]).then_inc(q["tr_ps"], 1)

            def values(s, h):
                pe.wait_ge(q["pT_ready"], 8 * s + h + 1)
                if h == 0:
                    wait(pe, q["oT_ready"], s)
                r = slice(32 * (h // 2), 32 * (h // 2) + 32)
                for b in range(GB):
                    c = (b * H0 + h) * 32
                    last = mm(O[r, b * N:(b + 1) * N], vpad[:, c:c + 32], g(pT0[:, h % 2, :], b),
                              start=(h % 2 == 0 and b == 0), stop=(h % 2 == 1), skip_group_check=True)
                last.then_inc(q["pv_ps"], 1)

            def project_out(s):
                pe.wait_ge(q["oT_ready"], s + 1)
                for b in range(GB):
                    last = mm(g(T, b), g(oT, b), wm[:, WO:WO + N], start=True, stop=True)
                last.then_inc(q["wo_ps"], 1)

            def tap(t):
                return wm[:, WC2 + t * N:WC2 + (t + 1) * N]

            def products(slot, src, weights, start=False):
                for c, w in enumerate(weights):
                    last = mm(phases(M[:, 1, :])[:, slot], w,
                              src[:, :, c:c + Q], start=(start and c == 0), stop=True, skip_group_check=True)
                return last

            def conv(m, i):
                ws = [[wsum[:, j, c, :] for c in range(4)] for j in range(5)]
                if i == 2:
                    pe.wait_ge(q["hp_ready"], m + 1)
                    products(2, xs[:, 5], ws[2] + [tap(16)], start=True)
                    products(3, xs[:, 5], ws[2] + [tap(16)])
                if i == 3:
                    pe.wait_ge(q["x2_ready"], m + 1)
                    products(0, xs[:, 3], ws[4])
                    products(1, xs[:, 1], ws[3] + [tap(16)])
                    products(2, xd[:, 2], ws[0] + [tap(16)])
                    products(3, xf[:, 2], ws[1]).then_inc(q["cp_ps"], 1)
                if i == 4:
                    pe.wait_ge(q["v2_done"], m + 1)
                    products(0, xd[:, 1], [tap(4 * c + 1) for c in range(4)], start=True)
                    products(1, xf[:, 1], [tap(4 * c + 3) for c in range(4)])
                if i == 5:
                    products(2, xd[:, 0], [tap(4 * c) for c in range(5)])
                    products(3, xf[:, 0], [tap(4 * c + 2) for c in range(4)]).then_inc(q["c2_ps"], 1)

            def gate(bank, j, parts, done):
                for n, (w, src) in enumerate(parts):
                    last = mm(M[:, bank, :], wm[:, w + j * N:w + (j + 1) * N], src[:, :],
                              start=(n == 0), stop=(n == len(parts) - 1))
                last.then_inc(q[done], 1)

            def layer1(m, i):
                if i == 0:
                    pe.wait_ge(ln_out[0], m + 1)
                    wait(pe, q["g2_done"], m)
                    transpose4(M[:, 0, :], x1).then_inc(q["x1t_ps"], 1)
                if i == 1:
                    pe.wait_ge(q["x1T_ready"], m + 1)
                    wait(pe, ln_out[1], m)
                    mm(M[:, 1, :], wm[:, W1:W1 + N], x1T[:, :], start=True, stop=True).then_inc(q["c1_ps"], 1)
                    mm(M[0:KS, 0, :], wse_s[:, :], x1T[:, :], start=True, stop=True).then_inc(q["d_ps"], 1)
                if i == 2:
                    pe.wait_ge(q["dd_ready"], m + 1)
                    for b in range(GB):
                        last = mm(g(M[:, 0, :], b), g(x1T, b), wm[:, WM:WM + N], start=True, stop=True)
                    last.then_inc(q["msg_ps"], 1)
                if i == 3:
                    pe.wait_ge(q["lr_done"], m + 1)
                    pe.wait_ge(q["m1_done"], m + 1)
                    for b in range(GB):
                        last = mm(g(M[:, 0, :], b), g(ll, b), g(lr, b), start=True, stop=True)
                    last.then_inc(q["arg_ps"], 1)
                conv(m, i)
                if i == 6:
                    pe.wait_ge(q["aT_done"], m + 1)
                    pe.wait_ge(q["msg_ready"], m + 1)
                    for b in range(GB):
                        last = mm(g(M[:, 0, :], b), g(msg, b), g(aT, b), start=True, stop=True)
                    last.then_inc(q["nmp_ps"], 1)
                if i == 8:
                    pe.wait_ge(q["nmT_ready"], m + 1)
                    pe.wait_ge(q["xc_ready"], m + 1)
                    gate(1, 0, [(WHH, x1T), (WIC, xcT), (WIN, nmT)], "r_ps")
                    gate(0, 1, [(WHH, x1T), (WIC, xcT), (WIN, nmT)], "z_ps")
                if i == 9:
                    pe.wait_ge(q["tr_ready"], m + 1)
                    gate(1, 2, [(WHH, x1T)], "ghn_ps")
                    pe.wait_ge(q["tz_ready"], m + 1)
                    gate(0, 2, [(WIC, xcT), (WIN, nmT)], "gin_ps")
                if i == 12:
                    pe.wait_ge(q["y_done"], m + 1)
                    transpose4(M[:, 1, :], yT).then_inc(q["yt_ps"], 1)

            def layers23(t, i, p, l0):
                u = t - 2
                if i == 0:
                    pe.wait_ge(ln_out[1], u + 1)
                    wait(pe, q["r3_done"], u)
                    transpose4(L[:, 0, :], x2).then_inc(q["x2t_ps"], 1)
                if i == 1:
                    pe.wait_ge(q["x2T_ready"], u + 1)
                    for b in range(GB):
                        c = (b % 2) * HC
                        last = mm(L[:, b // 2, c:c + HC], g(x2T, b), l2w[:, :], start=True, stop=True)
                    last.then_inc(q["h2_ps"], 1)
                if i == 3:
                    pe.wait_ge(q["hg_done"], u + 1)
                    for b in range(GB):
                        c = (b % 2) * HC
                        last = mm(L[:, b // 2, c:c + HC], g(at[p], b), hg[:, b, :], start=True, stop=True)
                    last.then_inc(q["num_ps"], 1)
                if i == 5:
                    pe.wait_ge(ln_out[2], u + 1)
                    transpose4(L[:, 0, :], x3).then_inc(q["x3t_ps"], 1)
                if i == 6:
                    pe.wait_ge(q["x3T_ready"], u + 1)
                    for b in range(GB):
                        c = (b % 2) * GC
                        last = mm(L[:, b // 2, c:c + GC], g(x3T, b), l3w[:, :], start=True, stop=True)
                    last.then_inc(q["h3_ps"], 1)
                if 9 <= i < 9 + H3:
                    h = i - 9
                    pe.wait_ge(q["p3_ready"], H3 * u + h + 1)
                    if l0 and h == 0:
                        pe.wait_ge(q["sc_ready"], H0 * t + H0)
                    if h >= 2:
                        pe.wait_ge(q["pT3_ready"], H3 * u + h - 1)
                    transpose4(S[h % 2], p3[:, h % 2, :]).then_inc(q["tr3_ps"], 1)
                if 7 <= i < 7 + H3:
                    h = i - 7
                    if h == 0:
                        pe.wait_ge(q["h3_ready"], u + 1)
                        pe.wait_ge(q["mask3_ready"], u + 1)
                    else:
                        pe.wait_ge(q["z3_ready"], H3 * u + h)
                    mm(L[:, 0, :], wa2b[:, h, :], x3T[:, :], start=True, stop=False)
                    mm(L[:, 0, :], identb[:, :], mask3[p][:, :], start=False, stop=True)\
                        .then_inc(q["e3_ps"], 1)
                if 9 <= i < 9 + H3:
                    h = i - 9
                    pe.wait_ge(q["pT3_ready"], H3 * u + h + 1)
                    for b in range(GB):
                        last = mm(L[32 * h:32 * h + 32, 1, b * N:(b + 1) * N], h3[:, b, h * D3:(h + 1) * D3],
                                  g(pT3[:, h % 2, :], b), start=(b == 0), stop=True, skip_group_check=True)
                    last.then_inc(q["pv3_ps"], 1)

            def layer3_out(u):
                pe.wait_ge(q["o3T_ready"], u + 1)
                pe.wait_ge(q["z3_ready"], H3 * u + H3)
                transpose4(L[:, 0, :], o3T).then_inc(q["o3n_ps"], 1)

            def step(k, p, l0, l1, l23):
                t = 2 * k + p
                for i in range(SLOTS):
                    if l0:
                        if i == 0:
                            project(t, p, k)
                        if 0 <= i - 1 < H0:
                            scores(t, i - 1)
                        if 0 <= i - 3 < H0:
                            probs_T(t, i - 3)
                    if l1:
                        layer1(t - 1, i)
                    if l23:
                        layers23(t, i, p, l0)
                    if l0:
                        if 0 <= i - 3 < H0:
                            values(t, i - 3)
                        if i == H0 + 3:
                            project_out(t)
                    if l23 and i == SLOTS - 1:
                        layer3_out(t - 2)

            steps(pe, step)

        @block.scalar
        def _(act):
            fn = nc.scalar.activation

            def project(s, p, k):
                act.wait_ge(q["q_ps"], s + 1)
                wait(act, q["qk_ps"], 8 * s)
                fn(qT[:, :], S[0][:, :], ACT.Copy, scale=float(D0) ** -0.5).then_inc(q["qT_ready"], 1)
                act.wait_ge(q["k_ps"], s + 1)
                wait(act, q["kh_ready"], 8 * s)
                fn(kT[:, :], S[1][:, :], ACT.Copy).then_inc(q["kT_ready"], 1)
                act.wait_ge(q["v_ps"], s + 1)
                wait(act, q["pv_ps"], 8 * s)
                src = T[:, :].rearrange("p (m e d) -> p m e d", e=2, d=D0)
                dst = vpad[:, :].rearrange("p (m e f d) -> p m e f d", e=2, f=2, d=D0)
                fn(dst[:, :, 0, 0, :], src[:, :, 0, :], ACT.Copy)
                fn(dst[:, :, 1, 1, :], src[:, :, 1, :], ACT.Copy).then_inc(q["v_ready"], 1)

            def exps(s, h):
                act.wait_ge(q["nm_ready"], 8 * s + h + 1)
                wait(act, q["p_ready"], 8 * s + h - 1)
                for b in range(GB):
                    last = fn(g(e0[:, h % 2, :], b), g(sc0[:, h % 2, :], b), ACT.Exp, bias=nm0[:, h % 2, b:b + 1],
                              accum_out=sum0[:, h % 2, b:b + 1])
                last.then_inc(q["exp_done"], 1)

            def probs_T(s, h):
                act.wait_ge(q["tr_ps"], 8 * s + h + 1)
                wait(act, q["pv_ps"], 8 * s + h - 1)
                fn(pT0[:, h % 2, :], T[:, :], ACT.Copy).then_inc(q["pT_ready"], 1)

            def layer1(m, i):
                if i == 0:
                    act.wait_ge(q["x1t_ps"], m + 1)
                    wait(act, q["y_done"], m)
                    fn(x1T[:, :], M[:, 0, :], ACT.Copy).then_inc(q["x1T_ready"], 1)
                if i == 1:
                    act.wait_ge(q["c1_ps"], m + 1)
                    wait(act, q["c2_ps"], m)
                    fn(xs[:, 4:8, :, PAD // 4:PAD // 4 + Q],
                       phases(M[:, 1, :]), ACT.Relu, bias=bnb[:, 0:1], scale=bns[:, 0:1])\
                        .then_inc(q["hp_ready"], 1)
                    act.wait_ge(q["d_ps"], m + 1)
                    wait(act, q["lr_done"], m)
                    fn(dd[:, :], M[0:KS, 0, :], ACT.Identity, bias=bse_s[:, :]).then_inc(q["dd_ready"], 1)
                if i == 2:
                    act.wait_ge(q["dd_ready"], m + 1)
                    fn(sql[:, :], dd[:, :], ACT.Square, scale=sel[:, 2:3], bias=sel[:, 1:2])
                    fn(sqr[:, :], dd[:, :], ACT.Square, scale=sel[:, 1:2], bias=sel[:, 2:3])\
                        .then_inc(q["sq_ready"], 1)
                    act.wait_ge(q["m1_done"], m + 1)
                    wait(act, q["nmp_ps"], m)
                    fn(msg[:, :], m1[:, :], ACT.Relu).then_inc(q["msg_ready"], 1)
                if i == 3:
                    act.wait_ge(q["arg_ps"], m + 1)
                    wait(act, q["aT_done"], m)
                    fn(em[:, :], M[:, 0, :], ACT.Exp).then_inc(q["em_ready"], 1)
                if i == 7:
                    act.wait_ge(q["nmp_ps"], m + 1)
                    wait(act, q["gin_ps"], m)
                    fn(nmT[:, :], M[:, 0, :], ACT.Copy).then_inc(q["nmT_ready"], 1)
                    act.wait_ge(q["u_done"], m + 1)
                    fn(xcT[:, :], u1[:, :], ACT.Relu, bias=bnb[:, 1:2]).then_inc(q["xc_ready"], 1)
                if i == 8:
                    act.wait_ge(q["r_ps"], m + 1)
                    wait(act, q["rr_done"], m)
                    fn(tr[:, :], M[:, 1, :], ACT.Tanh, bias=gb[:, 0:1], scale=0.5).then_inc(q["tr_ready"], 1)
                    act.wait_ge(q["z_ps"], m + 1)
                    wait(act, q["zd_done"], m)
                    fn(tz[:, :], M[:, 0, :], ACT.Tanh, bias=gb[:, 1:2], scale=0.5).then_inc(q["tz_ready"], 1)
                if i == 10:
                    act.wait_ge(q["g2_done"], m + 1)
                    wait(act, q["dx_done"], m)
                    fn(nT[:, :], g2[:, :], ACT.Tanh, bias=col[:, C_BIN:C_BIN + 1]).then_inc(q["n_ready"], 1)

            def layers23(u, i):
                if i == 0:
                    act.wait_ge(q["x2t_ps"], u + 1)
                    wait(act, q["h2_ps"], u)
                    fn(x2T[:, :], L[:, 0, :], ACT.Copy).then_inc(q["x2T_ready"], 1)
                if i == 1:
                    act.wait_ge(q["hb_done"], u + 1)
                    wait(act, q["wr_done"], u)
                    fn(eg[:, :, :], h2[:, :, N:HC], ACT.Exp).then_inc(q["eg_ready"], 1)
                if i == 5:
                    act.wait_ge(q["x3t_ps"], u + 1)
                    wait(act, q["e3_ps"], H3 * u)
                    fn(x3T[:, :], L[:, 0, :], ACT.Copy).then_inc(q["x3T_ready"], 1)
                if i == 6:
                    act.wait_ge(q["h3_ps"], u + 1)
                    wait(act, q["pv3_ps"], H3 * u)
                    fn(h3[:, :, :].rearrange("p (a b) c -> p a (b c)", a=2), L[:, 0:2, 0:2 * GC], ACT.Copy)\
                        .then_inc(q["h3_ready"], 1)
                if 9 <= i < 9 + H3:
                    h = i - 9
                    act.wait_ge(q["tr3_ps"], H3 * u + h + 1)
                    wait(act, q["pv3_ps"], H3 * u + h - 1)
                    fn(pT3[:, h % 2, :], S[h % 2][:, :], ACT.Copy).then_inc(q["pT3_ready"], 1)

                if 7 <= i < 7 + H3:
                    h = i - 7
                    if h == 0:
                        act.wait_ge(q["h3_ready"], u + 1)
                    act.wait_ge(q["e3_ps"], H3 * u + h + 1)
                    wait(act, q["l3_done"], H3 * u + h - 1)
                    for b in range(GB):
                        last = fn(g(z3[:, h % 2, :], b), g(L[:, 0, :], b), ACT.Identity,
                                  bias=h3[:, b, N + h:N + h + 1])
                    last.then_inc(q["z3_ready"], 1)
                if 8 <= i < 8 + H3:
                    h = i - 8
                    act.wait_ge(q["nm3_ready"], H3 * u + h + 1)
                    wait(act, q["p3_ready"], H3 * u + h - 1)
                    for b in range(GB):
                        last = fn(g(e3[:, h % 2, :], b), g(l3[:, h % 2, :], b), ACT.Exp,
                                  bias=nm3[:, h % 2, b:b + 1], accum_out=sum3[:, h % 2, b:b + 1])
                    last.then_inc(q["exp3_done"], 1)
            act.wait_ge(q["prep"], 1)

            def step(k, p, l0, l1, l23):
                t = 2 * k + p
                for i in range(SLOTS):
                    if l0:
                        if i == 0:
                            project(t, p, k)
                        if 0 <= i - 2 < H0:
                            exps(t, i - 2)
                        if 0 <= i - 3 < H0:
                            probs_T(t, i - 3)
                        if i == H0 + 3:
                            act.wait_ge(q["pv_ps"], 8 * t + 8)
                            wait(act, q["wo_ps"], t)
                            fn(oT[:, :], O[:, :], ACT.Copy).then_inc(q["oT_ready"], 1)
                    if l1:
                        layer1(t - 1, i)
                    if l23:
                        layers23(t - 2, i)
                    if l23 and i == SLOTS - 1:
                        u = t - 2
                        act.wait_ge(q["pv3_ps"], H3 * u + H3)
                        wait(act, q["o3n_ps"], u)
                        fn(o3T[:, :], L[:, 1, :], ACT.Copy).then_inc(q["o3T_ready"], 1)

            steps(act, step)

        @block.vector
        def _(dve):
            v = nc.vector
            dve.wait_ge(q["bn2_"], 1)
            v.tensor_tensor(bns[:, 0:1], bns[:, 0:1], col[:, C_G1:C_G1 + 1], ALU.mult)
            v.tensor_tensor(bns[:, 1:2], bns[:, 1:2], col[:, C_G2:C_G2 + 1], ALU.mult).then_inc(q["bn3_"], 1)
            dve.wait_ge(q["bn3_"], 1)
            v.tensor_tensor(bnt[:, 0:1], bns[:, 0:1], col[:, C_M1:C_M1 + 1], ALU.mult)
            v.tensor_tensor(bnt[:, 1:2], bns[:, 1:2], col[:, C_M2:C_M2 + 1], ALU.mult).then_inc(q["bn3_"], 1)
            v.tensor_tensor(gb[:, :], col[:, C_BIR:C_BIZ + 1], col[:, C_BHR:C_BHZ + 1], ALU.add)\
                .then_inc(q["bn4_"], 1)
            dve.wait_ge(q["bn3_"], 2)
            v.tensor_tensor(bnb[:, 0:1], col[:, C_B1:C_B1 + 1], bnt[:, 0:1], ALU.subtract)
            v.tensor_tensor(bnb[:, 1:2], col[:, C_B2:C_B2 + 1], bnt[:, 1:2], ALU.subtract)
            dve.wait_ge(q["bn4_"], 1)
            v.tensor_scalar(gb[:, :], gb[:, :], 0.5, None, ALU.mult)
            dve.wait_ge(q["rows_ps"], 1)
            v.tensor_copy(rowb[:, 0:H0 + 2 * N], M[:, 0, 0:H0 + 2 * N])
            dve.wait_ge(q["brow_ps"], 1)
            v.tensor_copy(brow[:, :], M[0:1, 1, 0:2]).then_inc(q["bn4_"], 1)
            dve.wait_ge(q["bn4_"], 2)
            v.tensor_tensor(brow[:, 0:1], brow[:, 0:1], row[:, R_AB:R_AB + 1], ALU.add).then_inc(q["brow_set"], 1)
            dve.wait_ge(q["wa_ps"], 1)
            v.tensor_copy(l2w[:, 0:N], wm[:, WL2:WL2 + N])
            v.tensor_copy(l2w[:, N:HC], L[:, 0, 0:2])
            v.tensor_copy(l3w[:, 0:N], wm[:, WL3:WL3 + N])
            v.tensor_copy(l3w[:, N:GC], S[0][:, 0:H3])
            v.tensor_copy(wa2[:, :], S[0][:, H3:2 * H3]).then_inc(q["wa_set"], 1)
            dve.wait_ge(q["wa_set"], 1)
            for h in range(H3):
                v.tensor_scalar(wa2b[:, h, :], ones[:, :], wa2[:, h:h + 1], None, ALU.mult)
            taps = wm[:, WC2:WC2 + 16 * N].rearrange("p (c j n) -> p j c n", j=4, n=N)
            for j, (a, b) in enumerate(((0, 1), (2, 3), (None, None), (0, 2), (1, 3))):
                if a is not None:
                    last = v.tensor_tensor(wsum[:, j], taps[:, a], taps[:, b], ALU.add)
            last.then_inc(q["wsum_set"], 1)
            dve.wait_ge(q["wsum_set"], 1)
            v.tensor_tensor(wsum[:, 2], wsum[:, 0], wsum[:, 1], ALU.add)
            dve.wait_ge(q["bl2_ps"], 1)
            dve.wait_ge(q["const_set"], 4)
            v.tensor_copy(rowb[:, H0 + 2 * N:H0 + 2 * N + 2], S[1][:, 0:2]).then_inc(q["prep"], 1)
            dve.wait_ge(q["prep"], 1)

            def layer_norm(i, u, src):
                for b in range(GB):
                    last = v.bn_stats(stats[i][:, b, :], g(src, b))
                last.then_inc(ln_stats[i], 1)
                dve.wait_ge(q["prep"], 1)
                dve.wait_ge(ln_stats[i], u + 1)
                for b in range(GB):
                    last = v.bn_aggr(meanv[i][:, b, :], stats[i][:, b, :])
                last.then_inc(ln_aggr[i], 1)

            def layer_norm_end(i, u, src, dst):
                dve.wait_ge(ln_rstd[i], u + 1)
                dve.wait_ge(ln_aggr[i], u + 1)
                for b in range(GB):
                    last = v.tensor_scalar(g(dst, b), g(src, b), meanv[i][:, b, 0:1], rstd[i][:, b:b + 1],
                                           ALU.subtract, ALU.mult)
                last.then_inc(ln_out[i], 1)

            def masks(s, p, k):
                dve.wait_ge(loaded[p], (k + 1) * 3 * DMA)
                wait(dve, q["qk_ps"], 8 * s)
                v.tensor_scalar(mask0[:, :], an[p][:, :], 0.0, NEG0, ALU.is_equal, ALU.mult)\
                    .then_inc(q["mask0_ready"], 1)

            def masks3(s, p):
                wait(dve, q["e3_ps"], H3 * (s - 1))
                v.tensor_scalar(mask3[p][:, :], an[p][:, :], 0.0, NEG3, ALU.is_le, ALU.mult)\
                    .then_inc(q["mask3_ready"], 1)

            def scores(s, h, p):
                dve.wait_ge(q["qk_ps"], 8 * s + h + 1)
                wait(dve, q["exp_done"], 8 * s + h - 1)
                v.scalar_tensor_tensor(out=sc0[:, h % 2, :], in0=an[p][:, :], scalar=we[:, h:h + 1],
                                       in1=S[h % 2][:, :], op0=ALU.mult, op1=ALU.add).then_inc(q["sc_ready"], 1)
                dve.wait_ge(q["sc_ready"], 8 * s + h + 1)
                v.tensor_reduce(nm0[:, h % 2, :], per(sc0[:, h % 2, :]), AX, ALU.max, negate=True)\
                    .then_inc(q["nm_ready"], 1)

            def norm(s, h):
                dve.wait_ge(q["exp_done"], 8 * s + h + 1)
                v.reciprocal(rec0[:, h % 2, :], sum0[:, h % 2, :]).then_inc(q["rec_done"], 1)
                dve.wait_ge(q["rec_done"], 8 * s + h + 1)
                wait(dve, q["tr_ps"], 8 * s + h - 1)
                v.tensor_tensor(per(p0[:, h % 2, :]), per(e0[:, h % 2, :]), wide(rec0[:, h % 2, :]), ALU.mult)\
                    .then_inc(q["p_ready"], 1)

            def front_end(s, p):
                dve.wait_ge(q["wo_ps"], s + 1)
                wait(dve, ln_out[0], s)
                v.tensor_tensor(r0[:, :], T[:, :], xn[p][:, :], ALU.add).then_inc(q["res0_done"], 1)
                dve.wait_ge(q["res0_done"], s + 1)
                layer_norm(0, s, r0)

            def layer1(m, i):
                if i == 2:
                    dve.wait_ge(q["msg_ps"], m + 1)
                    wait(dve, q["msg_ready"], m)
                    v.tensor_tensor(per(m1[:, :]), per(M[:, 0, :]),
                                    bmsg.unsqueeze(1).broadcast_to([128, GB, N]), ALU.add)\
                        .then_inc(q["m1_done"], 1)
                    dve.wait_ge(q["sq_ready"], m + 1)
                    dve.wait_ge(q["dd_ready"], m + 1)
                    wait(dve, q["arg_ps"], m)
                    v.scalar_tensor_tensor(out=lr[:, :], in0=dd[:, :], scalar=sel[:, 0:1], in1=sqr[:, :],
                                           op0=ALU.mult, op1=ALU.subtract)
                    v.scalar_tensor_tensor(out=ll[:, :], in0=dd[:, :], scalar=sel2[:, 0:1], in1=sql[:, :],
                                           op0=ALU.mult, op1=ALU.add).then_inc(q["lr_done"], 1)
                if i == 3:
                    dve.wait_ge(q["cp_ps"], m + 1)
                    dve.wait_ge(q["x1T_ready"], m + 1)
                    for c in range(4):
                        last = v.scalar_tensor_tensor(
                            out=phases(vT[:, :])[:, c], in0=phases(M[:, 1, :])[:, c // 2], scalar=bns[:, 1:2],
                            in1=phases(x1T[:, :])[:, c], op0=ALU.mult, op1=ALU.add)
                    last.then_inc(q["v1_done"], 1)
                    dve.wait_ge(q["v1_done"], m + 1)
                    for x in range(2):
                        half = vT[:, :].rearrange("p (b x n) -> p x b n", b=GB, x=2)[:, x]
                        last = v.scalar_tensor_tensor(
                            out=half, in0=M[:, 1, :].rearrange("p (b x n) -> p x b n", b=GB, x=2)[:, 1],
                            scalar=bns[:, 1:2], in1=half, op0=ALU.mult, op1=ALU.add)
                    last.then_inc(q["v2_done"], 1)
                if i == 6:
                    dve.wait_ge(q["c2_ps"], m + 1)
                    dve.wait_ge(q["v2_done"], m + 1)
                    wait(dve, q["xc_ready"], m)
                    v.scalar_tensor_tensor(out=u1[:, :], in0=M[:, 1, :], scalar=bns[:, 1:2], in1=vT[:, :],
                                           op0=ALU.mult, op1=ALU.add).then_inc(q["u_done"], 1)
                if i == 9:
                    dve.wait_ge(q["tr_ready"], m + 1)
                    v.tensor_scalar(rr[:, :], tr[:, :], 0.5, 0.5, ALU.mult, ALU.add).then_inc(q["rr_done"], 1)
                if i == 10:
                    dve.wait_ge(q["rr_done"], m + 1)
                    dve.wait_ge(q["ghn_ps"], m + 1)
                    v.scalar_tensor_tensor(out=g1[:, :], in0=M[:, 1, :], scalar=col[:, C_BHN:C_BHN + 1],
                                           in1=rr[:, :], op0=ALU.add, op1=ALU.mult).then_inc(q["g1_done"], 1)
                    dve.wait_ge(q["g1_done"], m + 1)
                    dve.wait_ge(q["gin_ps"], m + 1)
                    wait(dve, q["n_ready"], m)
                    v.tensor_tensor(g2[:, :], M[:, 0, :], g1[:, :], ALU.add).then_inc(q["g2_done"], 1)
                if i == 11:
                    dve.wait_ge(q["dx_done"], m + 1)
                    dve.wait_ge(q["tz_ready"], m + 1)
                    v.scalar_tensor_tensor(out=zd[:, :], in0=tz[:, :], scalar=1.0, in1=dx[:, :],
                                           op0=ALU.add, op1=ALU.mult).then_inc(q["zd_done"], 1)
                    dve.wait_ge(q["zd_done"], m + 1)
                    wait(dve, q["yt_ps"], m)
                    v.scalar_tensor_tensor(out=yT[:, :], in0=zd[:, :], scalar=0.5, in1=nx[:, :],
                                           op0=ALU.mult, op1=ALU.add).then_inc(q["y_done"], 1)
                if i == 12:
                    dve.wait_ge(q["yt_ps"], m + 1)
                    layer_norm(1, m, M[:, 1, :])
                if i == 13:
                    wait(dve, q["x2t_ps"], m)
                    wait(dve, q["r2_done"], m)
                    layer_norm_end(1, m, M[:, 1, :], x2)

            def layers23(u, i):
                if i == 1:
                    dve.wait_ge(q["h2_ps"], u + 1)
                    wait(dve, q["hg_done"], u)
                    for a in range(2):
                        last = v.tensor_tensor(h2[:, 2 * a:2 * a + 2, :],
                                               L[:, a, 0:2 * HC].rearrange("p (b c) -> p b c", c=HC),
                                               bl2.unsqueeze(1).broadcast_to([128, 2, HC]), ALU.add)
                    last.then_inc(q["hb_done"], 1)
                if i == 2:
                    dve.wait_ge(q["hb_done"], u + 1)
                    dve.wait_ge(q["eg_ready"], u + 1)
                    wait(dve, q["num_ps"], u)
                    v.tensor_tensor(hg[:, :, 0:N], h2[:, :, 0:N], wide(eg[:, :, 1]), ALU.mult)
                    v.tensor_copy(hg[:, :, N:HC], eg[:, :, 1:2].broadcast_to([128, GB, 2])).then_inc(q["hg_done"], 1)
                if i == 3:
                    num = L[:, 0:2, 0:2 * HC].rearrange("p a (b c) -> p a b c", c=HC)
                    dve.wait_ge(q["num_ps"], u + 1)
                    v.tensor_tensor(dn[:, :].rearrange("p (a b) -> p a b", a=2), num[:, :, :, N],
                                    eg[:, :, 0].rearrange("p (a b) -> p a b", a=2), ALU.mult)\
                        .then_inc(q["dn_done"], 1)
                    dve.wait_ge(q["dn_done"], u + 1)
                    v.reciprocal(rdn[:, :], dn[:, :]).then_inc(q["rdn_done"], 1)
                    dve.wait_ge(q["rdn_done"], u + 1)
                    v.tensor_tensor(wr[:, :], rdn[:, :], eg[:, :, 0], ALU.mult).then_inc(q["wr_done"], 1)
                    dve.wait_ge(q["wr_done"], u + 1)
                    dve.wait_ge(ln_out[1], u + 1)
                    wait(dve, ln_out[2], u)
                    for b in range(GB):
                        last = v.scalar_tensor_tensor(out=g(r2, b), in0=num[:, b // 2, b % 2, 0:N],
                                                      scalar=wr[:, b:b + 1], in1=g(x2, b),
                                                      op0=ALU.mult, op1=ALU.add)
                    last.then_inc(q["r2_done"], 1)
                    dve.wait_ge(q["r2_done"], u + 1)
                    layer_norm(2, u, r2)
                if i == 4:
                    wait(dve, q["x3t_ps"], u)
                    wait(dve, q["r3_done"], u)
                    layer_norm_end(2, u, r2, x3)
                if 8 <= i < 8 + H3:
                    h = i - 8
                    dve.wait_ge(q["exp3_done"], H3 * u + h + 1)
                    v.reciprocal(rec3[:, h % 2, :], sum3[:, h % 2, :]).then_inc(q["rec3_done"], 1)
                    dve.wait_ge(q["rec3_done"], H3 * u + h + 1)
                    wait(dve, q["tr3_ps"], H3 * u + h - 1)
                    v.tensor_tensor(per(p3[:, h % 2, :]), per(e3[:, h % 2, :]), wide(rec3[:, h % 2, :]),
                                    ALU.mult).then_inc(q["p3_ready"], 1)

                if 7 <= i < 7 + H3:
                    h = i - 7
                    dve.wait_ge(q["z3_ready"], H3 * u + h + 1)
                    wait(dve, q["exp3_done"], H3 * u + h - 1)
                    v.scalar_tensor_tensor(out=l3[:, h % 2, :], in0=z3[:, h % 2, :], scalar=SLOPE,
                                           in1=z3[:, h % 2, :], op0=ALU.mult, op1=ALU.max)\
                        .then_inc(q["l3_done"], 1)
                    dve.wait_ge(q["l3_done"], H3 * u + h + 1)
                    v.tensor_reduce(nm3[:, h % 2, :], per(l3[:, h % 2, :]), AX, ALU.max, negate=True)\
                        .then_inc(q["nm3_ready"], 1)
            def step(k, p, l0, l1, l23):
                t = 2 * k + p
                for i in range(SLOTS):
                    if l0:
                        if i == 0:
                            masks(t, p, k)
                        if 0 <= i - 1 < H0:
                            scores(t, i - 1, p)
                        if 0 <= i - 2 < H0:
                            norm(t, i - 2)
                    if l1:
                        layer1(t - 1, i)
                    if l23:
                        layers23(t - 2, i)
                    if l0:
                        if i == H0 + 3:
                            front_end(t, p)
                        if i == H0 + 4:
                            wait(dve, q["x1t_ps"], t)
                            layer_norm_end(0, t, r0, x1)
                            masks3(t, p)
                    if l23 and i == SLOTS - 1:
                        u = t - 2
                        dve.wait_ge(q["o3n_ps"], u + 1)
                        dve.wait_ge(ln_out[2], u + 1)
                        wait(dve, ln_out[3], u)
                        v.tensor_tensor(r3[:, :], L[:, 0, :], x3[:, :], ALU.add).then_inc(q["r3_done"], 1)
                        dve.wait_ge(q["r3_done"], u + 1)
                        layer_norm(3, u, r3)
                        wait(dve, stored[p], (k - 1) * DMA)
                        layer_norm_end(3, u, r3, xo[p])

            steps(dve, step)


SLOTS = 14


def kernel(**inputs):
    import numpy as np
    import concourse.bacc as bacc
    from concourse.bass_utils import run_bass_kernel_spmd

    i = {n: np.ascontiguousarray(a) for n, a in inputs.items()}
    flat = lambda a: np.ascontiguousarray(a.reshape(N, -1))
    wih = i["L1_gnn_w_ih"].T
    order = np.arange(N).reshape(Q, 2, 2).transpose(2, 1, 0)[::-1].reshape(N)
    x, adj = i["x"][:, order], i["adj"][:, order][:, :, order]
    mats = np.concatenate(
        [i["L0_gnn_W_q"].T, i["L0_gnn_W_k"].T, i["L0_gnn_W_v"].T, i["L0_gnn_W_o"].T,
         i["L1_gnn_conv1_w"][:, :, 0].T, i["L1_gnn_w_msg"].T, i["L2_gnn_W_w"].T, i["L2_gnn_W_w"],
         i["L3_gnn_W"], i["L3_gnn_W"].T, i["L1_gnn_w_hh"].T, wih[0:N], wih[N:2 * N],
         i["L1_gnn_conv2_w"].transpose(1, 2, 0).reshape(N, TAPS * N)], axis=1)
    bih, bhh = i["L1_gnn_b_ih"], i["L1_gnn_b_hh"]
    cols = np.stack(
        [i["L1_gnn_bn1_g"], i["L1_gnn_bn1_b"], i["L1_gnn_bn1_m"], i["L1_gnn_bn1_v"],
         i["L1_gnn_bn2_g"], i["L1_gnn_bn2_b"], i["L1_gnn_bn2_m"], i["L1_gnn_bn2_v"],
         bih[0:N], bih[N:2 * N], bih[2 * N:], bhh[0:N], bhh[N:2 * N], bhh[2 * N:],
         i["L2_gnn_a_w"][0:N], i["L2_gnn_a_w"][N:], i["L2_gnn_W_b"]], axis=1)
    rows = np.concatenate([i["L0_gnn_W_e"][:, 0], i["L1_gnn_b_msg"], i["L2_gnn_W_b"], i["L2_gnn_a_b"]])[None, :]
    arrays = {
        "x_n": flat(x.transpose(1, 0, 2)), "x_t": flat(x.transpose(2, 0, 1)),
        "adj_n": flat(adj.transpose(1, 0, 2)), "adj_t": flat(adj.transpose(2, 0, 1)),
        "mats": np.ascontiguousarray(mats),
        "wse": np.ascontiguousarray(np.concatenate([i["L1_gnn_w_se"].T] * 3, axis=1)),
        "cols": np.ascontiguousarray(cols), "rows": np.ascontiguousarray(rows),
        "bse": np.ascontiguousarray(np.concatenate([i["L1_gnn_b_se"]] * 3)[:, None]),
        "att3": i["L3_gnn_a"],
    }
    nc = bacc.Bacc("TRN2", target_bir_lowering=False, num_devices=1)
    args = [nc.dram_tensor(f"in_{n}", a.shape, F32, kind="ExternalInput").ap() for n, a in arrays.items()]
    out = nc.dram_tensor("out_x", (N, N * N), F32, kind="ExternalOutput").ap()
    build(nc, *args, out)
    r = run_bass_kernel_spmd(nc, [{f"in_{n}": a for n, a in arrays.items()}], core_ids=[0])
    return np.ascontiguousarray(r.results[0]["out_x"].reshape(N, N, N).transpose(1, 0, 2)[:, np.argsort(order)])
```

```python
from contextlib import ExitStack

import concourse.bass as bass
from concourse import mybir

F32 = mybir.dt.float32
BF16 = mybir.dt.bfloat16
ALU = mybir.AluOpType
ACT = mybir.ActivationFunctionType
AX = mybir.AxisListType.X

N = 128
GB = 4
W = GB * N
GROUPS = N // GB
H0, D0 = 8, 16
H3, D3 = 4, 32
TAPS, PAD = 17, 8
Q = N // 4
QP = Q + PAD // 2
EPS = 1e-5
NEG0 = -1.0e30
NEG3 = -9.0e15
SLOPE = 0.2
NS = 3
KS = 3 * NS
HC = N + 2
GC = N + H3
DMA = 16

(C_G1, C_B1, C_M1, C_V1, C_G2, C_B2, C_M2, C_V2, C_BIR, C_BIZ, C_BIN, C_BHR, C_BHZ, C_BHN, C_A1, C_A2,
 C_WB) = range(17)
NCOL = 17
R_WE, R_BM, R_WB, R_AB = 0, H0, H0 + N, H0 + 2 * N
NROW = H0 + 2 * N + 1
WQ, WK, WV, WO, W1, WM, WL2, WL2N, WL3, WL3T, WHH = (N * i for i in range(11))
WIC, WIN, WC2 = N * 13, N * 16, N * 19
NMAT = N * (19 + TAPS)


def build(nc, x_n, x_t, adj_n, adj_t, mats, wse, cols, rows, bse, att3, out):
    with ExitStack() as ctx:
        def sb(name, shape, dt=F32):
            return ctx.enter_context(nc.sbuf_tensor(name, shape, dt))

        def ps(name, shape, dt=F32):
            return ctx.enter_context(nc.psum_tensor(name, shape, dt))

        def sem(name):
            return ctx.enter_context(nc.semaphore(name))

        wm = sb("wm", [128, NMAT])
        col = sb("col", [128, NCOL])
        row = sb("row", [1, NROW])
        wse_s = sb("wse_s", [128, KS])
        bse_s = sb("bse_s", [KS, 1])
        att = sb("att", [128, 2 * H3])
        ident = sb("ident", [128, 128])
        identb = sb("identb", [128, 128], BF16)
        ones = sb("ones", [128, 128])
        headm = sb("headm", [128, H0])
        sel = sb("sel", [KS, 4])
        sel2 = sb("sel2", [KS, 1])
        neghalf = sb("neghalf", [128, GB])
        eps4 = sb("eps4", [128, GB])
        bns = sb("bns", [128, 2])
        bnt = sb("bnt", [128, 2])
        bnb = sb("bnb", [128, 2])
        gb = sb("gb", [128, 2])
        rowb = sb("rowb", [128, H0 + 2 * N + 2])
        brow = sb("brow", [1, 2])
        l2w = sb("l2w", [128, HC])
        l3w = sb("l3w", [128, GC])
        wa2 = sb("wa2", [128, 96])
        seljb = sb("seljb", [96, H3, 128], BF16)
        we = rowb[:, 0:H0]
        bmsg = rowb[:, H0:H0 + N]
        bl2 = rowb[:, H0 + N:H0 + 2 * N + 2]

        xn = [sb(f"xn{p}", [128, W]) for p in range(2)]
        xt = [sb(f"xt{p}", [128, W]) for p in range(2)]
        an = [sb(f"an{p}", [128, W]) for p in range(2)]
        at = [sb(f"at{p}", [128, W]) for p in range(2)]
        mask3 = [sb(f"mask3{p}", [128, W], BF16) for p in range(2)]
        mask3_late = sb("mask3_late", [128, W], BF16)
        mask0 = sb("mask0", [128, W], BF16)
        qT = sb("qT", [128, W])
        kT = sb("kT", [128, W])
        kh = sb("kh", [128, H0, W])
        vpad = sb("vpad", [128, GB * H0 * 32])
        sc0 = sb("sc0", [128, 2, W])
        nm0 = sb("nm0", [128, 2, GB])
        e0 = sb("e0", [128, 2, W])
        sum0 = sb("sum0", [128, 2, GB])
        rec0 = sb("rec0", [128, 2, GB])
        p0 = sb("p0", [128, 2, W])
        pT0 = sb("pT0", [128, 2, W])
        oT = sb("oT", [128, W])
        r0 = sb("r0", [128, W])
        x1 = sb("x1", [128, W])
        x1T = sb("x1T", [128, W])
        xs = sb("xs", [128, 8, GB, QP])
        xd = sb("xd", [128, 3, GB, QP])
        xf = sb("xf", [128, 3, GB, QP])
        wsum = sb("wsum", [128, 5, 4, N])
        vT = sb("vT", [128, W])
        dd = sb("dd", [KS, W])
        sql = sb("sql", [KS, W])
        sqr = sb("sqr", [KS, W])
        ll = sb("ll", [KS, W])
        lr = sb("lr", [KS, W])
        msg = sb("msg", [128, W])
        em = sb("em", [128, W])
        aT = sb("aT", [128, W])
        u1 = sb("u1", [128, W])
        xcT = sb("xcT", [128, W])
        nmT = sb("nmT", [128, W])
        tr = sb("tr", [128, W])
        tz = sb("tz", [128, W])
        rr = sb("rr", [128, W])
        gn = sb("gn", [128, W])
        nT = sb("nT", [128, W])
        zplus = sb("zplus", [128, W])
        zx = sb("zx", [128, W])
        zn = sb("zn", [128, W])
        zminus = sb("zminus", [128, W])
        yT = sb("yT", [128, W])
        x2 = sb("x2", [128, W])
        x2T = sb("x2T", [128, W])
        h2 = sb("h2", [128, GB, HC])
        eg = sb("eg", [128, GB, 2])
        hg = sb("hg", [128, GB, HC])
        dn = sb("dn", [128, GB])
        rdn = sb("rdn", [128, GB])
        wr = sb("wr", [128, GB])
        r2 = sb("r2", [128, W])
        x3 = [sb(f"x3{p}", [128, W]) for p in range(2)]
        x3T = sb("x3T", [128, W])
        h3 = sb("h3", [128, GB, GC])
        ej = sb("ej", [96, W])
        ejr = sb("ejr", [64, W])
        ejb = sb("ejb", [96, W], BF16)
        z3 = sb("z3", [128, 2, W])
        l3 = sb("l3", [128, 2, W])
        nm3 = sb("nm3", [128, 2, GB])
        e3 = sb("e3", [128, 2, W])
        sum3 = sb("sum3", [128, 2, GB])
        rec3 = sb("rec3", [128, 2, GB])
        p3 = sb("p3", [128, 2, W])
        pT3 = sb("pT3", [128, 2, W])
        o3T = sb("o3T", [128, W])
        r3 = sb("r3", [128, W])
        selj = r3[0:96, :].rearrange("p (h n) -> p h n", h=H3)
        xo = [sb(f"xo{p}", [128, W]) for p in range(2)]
        stats = [sb(f"stats{i}", [128, GB, 6]) for i in range(4)]
        meanv = [sb(f"meanv{i}", [128, GB, 2]) for i in range(4)]
        veps = [sb(f"veps{i}", [128, GB]) for i in range(4)]
        rstd = [sb(f"rstd{i}", [128, GB]) for i in range(4)]

        S = [ps("S0", [128, W]), ps("S1", [128, W])]
        T = ps("T", [128, W])
        O = ps("O", [128, W])
        M = ps("M", [128, 2, W])
        L = ps("L", [128, 2, W])

        names = """wload wcol ones_set pads_set sel_set id_set const_set bn1_ bn2_ bn3_ bn4_ rows_ps brow_ps
            brow_set bl2_ps wa_ps prep q_ps k_ps v_ps qT_ready kT_ready v_ready mask0_ready
            mask3_ready mask3_kept oT_ready wo_ps res0_done x1t_ps x1T_ready c1_ps hp_ready x1_ready
            x2_ready wsum_set cp_ps v1_done v2_done d_ps dd_ready sq_ready lr_done msg_ps m1_done
            msg_ready c2_ps u_done xc_ready arg_ps em_ready aT_done nmp_ps nmT_ready ghn_ps r_ps
            tr_ready z_ps tz_ready gin_ps rr_done g1_done g2_done n_ready zx_done zp_done zn_done
            y_done yt_ps x2t_ps x2T_ready h2_ps hb_done eg_ready hg_done num_ps dn_done rdn_done
            wr_done r2_done x3t_ps x3T_ready h3_ps h3_ready ej_ps ej_ready ej_rest ej_middle ej_split
            selj_set o3T_ready o3n_ps r3_done""".split()
        per_head = """kh_ready qk_ps sc_ready nm_ready exp_done rec_done p_ready tr_ps pT_ready pv_ps
            e3_ps z3_ready l3_done nm3_ready exp3_done rec3_done p3_ready tr3_ps pT3_ready pv3_ps""".split()
        q = {n: sem(n) for n in names + per_head}
        loaded = [sem("loaded0"), sem("loaded1")]
        loaded_t = [sem("loaded_t0"), sem("loaded_t1")]
        stored = [sem("stored0"), sem("stored1")]
        ln_stats = [sem(f"ln_stats{i}") for i in range(4)]
        ln_aggr = [sem(f"ln_aggr{i}") for i in range(4)]
        ln_veps = [sem(f"ln_veps{i}") for i in range(4)]
        ln_rstd = [sem(f"ln_rstd{i}") for i in range(4)]
        ln_out = [sem(f"ln_out{i}") for i in range(4)]

        def g(t, b):
            return t[:, b * N:(b + 1) * N]

        def per(t):
            return t.rearrange("p (b n) -> p b n", b=GB)

        def phases(t):
            return t.rearrange("p (b c r) -> p c b r", b=GB, c=4)

        def wide(s):
            return s.unsqueeze(2).broadcast_to([128, GB, N])

        def wait(eng, s, value):
            if isinstance(value, int) and value <= 0:
                return
            eng.wait_ge(s, value)

        def phases_of(t):
            return [not isinstance(t, int) or 0 <= t - d < GROUPS for d in (0, 1, 2, 3, 4, -1)]

        def steps(eng, step):
            for t in range(6):
                step(t // 2, t % 2, phases_of(t))
            with eng.Fori(3, GROUPS // 2 - 1) as k:
                step(k, 0, [True] * 6)
                step(k, 1, [True] * 6)
            for t in range(GROUPS - 2, GROUPS + 4):
                step(t // 2, t % 2, phases_of(t))

        block = ctx.enter_context(nc.Block())

        @block.sync
        def _(sp):
            def load(t, p):
                for dst, src in ((xt, x_t), (an, adj_n), (xn, x_n)):
                    sp.dma_start(dst[p][:, :], src[:, bass.ds(t * W, W)]).then_inc(loaded[p], DMA)

            def load_t(t, p):
                sp.dma_start(at[p][:, :], adj_t[:, bass.ds(t * W, W)]).then_inc(loaded_t[p], DMA)

            def load_t_next(t, p):
                sp.wait_ge(q["num_ps"], t - 1)
                load_t(t, p)

            def load_next(t, p):
                sp.wait_ge(q["v_ps"], t + 1)
                sp.wait_ge(q["res0_done"], t + 1)
                sp.wait_ge(q["mask3_ready"], t + 1)
                load(t + 2, p)

            def store(t, p):
                sp.wait_ge(ln_out[3], t + 1)
                sp.dma_start(out[:, bass.ds(t * W, W)], xo[p][:, :]).then_inc(stored[p], DMA)

            sp.dma_start(wm[:, 0:WIC], mats[:, 0:WIC]).then_inc(q["wload"], DMA)
            load(0, 0)
            sp.dma_start(col[:, :], cols).then_inc(q["wcol"], DMA)
            sp.dma_start(row[:, :], rows).then_inc(q["wcol"], DMA)
            sp.dma_start(wse_s[:, :], wse).then_inc(q["wcol"], DMA)
            sp.dma_start(bse_s[:, :], bse).then_inc(q["wcol"], DMA)
            sp.wait_ge(q["pads_set"], 1)
            for h in range(H3):
                for j in range(2):
                    sp.dma_start(att[h * D3:(h + 1) * D3, j * H3 + h:j * H3 + h + 1],
                                 att3[h, j * D3:(j + 1) * D3].rearrange("(d o) -> d o", o=1))\
                        .then_inc(q["wcol"], DMA)
            sp.dma_start(wm[:, WIC:NMAT], mats[:, WIC:NMAT]).then_inc(q["wload"], DMA)
            load(1, 1)
            load_t(0, 0)
            load_t(1, 1)
            load_next(0, 0)
            load_next(1, 1)
            for t in (2, 3):
                load_t_next(t, t % 2)
                load_next(t, t % 2)
            store(0, 0)
            with sp.Fori(2, GROUPS // 2 - 1) as k:
                for p in range(2):
                    load_t_next(2 * k + p, p)
                    load_next(2 * k + p, p)
                    store(2 * k + p - 3, 1 - p)
            for t in (GROUPS - 2, GROUPS - 1):
                load_t_next(t, t % 2)
                store(t - 3, 1 - t % 2)
            for t in range(GROUPS - 3, GROUPS):
                store(t, t % 2)
            sp.wait_ge(stored[0], DMA * GROUPS // 2)
            sp.wait_ge(stored[1], DMA * GROUPS // 2)

        @block.gpsimd
        def _(pool):
            pool.memset(ones[:, :], 1.0).then_inc(q["ones_set"], 1)
            pool.memset(att[:, :], 0.0)
            pool.memset(wa2[:, :], 0.0)
            pool.memset(selj[:, :, :], 0.0).then_inc(q["selj_set"], 1)
            pool.memset(xs[:, :, :, :], 0.0)
            pool.memset(neghalf[:, :], -0.5)
            pool.memset(eps4[:, :], EPS)
            pool.memset(vpad[:, :], 0.0).then_inc(q["pads_set"], 1)
            pool.memset(sel[:, :], 1.0)
            pool.memset(ident[:, :], 0.0).then_inc(q["sel_set"], 1)
            pool.memset(headm[:, :], 1.0).then_inc(q["sel_set"], 1)
            pool.wait_ge(q["sel_set"], 2)
            pool.affine_select(out=ident[:, :], in_=ident[:, :], compare_op=ALU.not_equal, fill=1.0, base=0,
                               pattern=[[-1, 128]], channel_multiplier=1).then_inc(q["id_set"], 1)
            pool.affine_select(out=headm[:, :], in_=headm[:, :], compare_op=ALU.is_ge, fill=0.0, base=0,
                               pattern=[[-D0, H0]], channel_multiplier=1).then_inc(q["id_set"], 1)
            pool.affine_select(out=sel[:, :], in_=sel[:, :], compare_op=ALU.is_ge, fill=0.0, base=0,
                               pattern=[[-NS, 4]], channel_multiplier=1).then_inc(q["id_set"], 1)
            pool.wait_ge(q["id_set"], 3)
            pool.affine_select(out=headm[:, :], in_=headm[:, :], compare_op=ALU.is_ge, fill=0.0, base=D0 - 1,
                               pattern=[[D0, H0]], channel_multiplier=-1).then_inc(q["const_set"], 1)
            pool.affine_select(out=sel[:, :], in_=sel[:, :], compare_op=ALU.is_ge, fill=0.0, base=NS - 1,
                               pattern=[[NS, 4]], channel_multiplier=-1).then_inc(q["const_set"], 1)
            pool.tensor_copy(identb[:, :], ident[:, :]).then_inc(q["const_set"], 1)
            pool.wait_ge(q["const_set"], 2)
            pool.tensor_scalar(sel2[:, :], sel[:, 0:1], 2.0, 1.0, ALU.mult, ALU.mult).then_inc(q["const_set"], 1)
            for j in range(3):
                pool.wait_ge(q["selj_set"], j + 1)
                pool.affine_select(out=selj[:, :, :], in_=selj[:, :, :], compare_op=ALU.not_equal, fill=1.0,
                                   base=-32 * j, pattern=[[-1, H3], [0, 128]], channel_multiplier=1)\
                    .then_inc(q["selj_set"], 1)
            pool.wait_ge(q["selj_set"], 4)
            pool.tensor_copy(seljb[:, :, :], selj[:, :, :]).then_inc(q["selj_set"], 1)
            pool.wait_ge(q["wcol"], 12 * DMA)
            pool.wait_ge(q["const_set"], 4)
            for j, v in enumerate((C_V1, C_V2)):
                pool.tensor_scalar(bnt[:, j:j + 1], col[:, v:v + 1], EPS, 1.0, ALU.add, ALU.mult)\
                    .then_inc(q["bn1_"], 1)
            pool.wait_ge(q["bn1_"], 2)
            pool.tensor_tensor(bns[:, :], bnt[:, :], neghalf[:, 0:2], ALU.pow).then_inc(q["bn2_"], 1)

            def rsqrt(i, u):
                pool.wait_ge(ln_aggr[i], u + 1)
                pool.tensor_tensor(veps[i][:, :], meanv[i][:, :, 1], eps4[:, :], ALU.add)\
                    .then_inc(ln_veps[i], 1)
                pool.wait_ge(ln_veps[i], u + 1)
                pool.tensor_tensor(rstd[i][:, :], veps[i][:, :], neghalf[:, :], ALU.pow)\
                    .then_inc(ln_rstd[i], 1)

            def k_heads(s):
                wait(pool, q["qk_ps"], 8 * s)
                pool.wait_ge(q["kT_ready"], s + 1)
                pool.tensor_tensor(kh[:, 0, :], kT[:, :], headm[:, 0:1].broadcast_to([128, W]), ALU.mult)\
                    .then_inc(q["kh_ready"], 1)
            def k_heads_rest(s, heads):
                for h in heads:
                    pool.tensor_scalar(kh[:, h, :], kT[:, :], headm[:, h:h + 1], 1.0, ALU.mult, ALU.mult)\
                        .then_inc(q["kh_ready"], 1)

            def step(k, p, phases_now):
                l0, l1, l2, l3, l3e, ahead = phases_now
                t = 2 * k + p
                m, u = t - 1, t - 2
                if l3e:
                    rsqrt(3, t - 4)
                if l1:
                    pool.wait_ge(q["hp_ready"], m + 1)
                    wait(pool, q["c2_ps"], m)
                    e, o = xs[:, 6:8], xs[:, 4:6]
                    tt = pool.tensor_tensor
                    tt(xs[:, 0:2].rearrange("p y b i -> p (y b i)"), e.rearrange("p y b i -> p (y b i)"),
                       o.rearrange("p y b i -> p (y b i)"), ALU.subtract)
                    tt(xs[:, 2], e[:, 1], o[:, 0], ALU.subtract)
                    tt(xs[:, 3, :, 0:QP - 1], e[:, 0, :, 1:QP], o[:, 1, :, 0:QP - 1], ALU.subtract)\
                        .then_inc(q["x1_ready"], 1)
                    pool.wait_ge(q["x1_ready"], m + 1)
                    x2l = xs[:, 0:6].rearrange("p (k y) b i -> p k y b i", y=2)
                    tt(xd[:, :, :, :], x2l[:, :, 0], x2l[:, :, 1], ALU.subtract)
                    tt(xf[:, :, :, 0:QP - 1], x2l[:, :, 0, :, 1:QP], x2l[:, :, 1, :, 0:QP - 1], ALU.subtract)\
                        .then_inc(q["x2_ready"], 1)
                if l1:
                    pool.wait_ge(loaded_t[1 - p], (k + p) * DMA)
                    pool.wait_ge(q["em_ready"], m + 1)
                    wait(pool, q["nmp_ps"], m)
                    pool.tensor_tensor(aT[:, :], em[:, :], at[1 - p][:, :], ALU.mult).then_inc(q["aT_done"], 1)
                if l3:
                    n = t - 2
                    pool.wait_ge(q["ej_ready"], n)
                    pool.tensor_tensor(ejr[:, :], ej[0:64, :], ejb[0:64, :], ALU.subtract)\
                        .then_inc(q["ej_rest"], 1)
                    pool.wait_ge(q["const_set"], 4)
                    pool.wait_ge(q["ej_rest"], n)
                    pool.tensor_scalar(ejb[0:64, :], ejr[:, :], 1.0, 1.0, ALU.mult, ALU.mult)\
                        .then_inc(q["ej_middle"], 1)
                    pool.wait_ge(q["ej_middle"], n)
                    pool.tensor_tensor(ejb[0:32, :], ejr[0:32, :], ejb[0:32, :], ALU.subtract)\
                        .then_inc(q["ej_split"], 1)
                if l2:
                    rsqrt(2, u)
                if l1:
                    pool.wait_ge(q["const_set"], 4)
                    pool.wait_ge(q["tz_ready"], m + 1)
                    wait(pool, q["y_done"], m)
                    pool.tensor_scalar(zplus[:, :], tz[:, :], 0.5, 1.5, ALU.mult, ALU.add).then_inc(q["zp_done"], 1)
                    pool.tensor_scalar(zminus[:, :], tz[:, :], -0.5, 0.5, ALU.mult, ALU.add).then_inc(q["zp_done"], 1)
                    pool.wait_ge(q["zp_done"], 2 * m + 1)
                    pool.tensor_tensor(zx[:, :], zplus[:, :], x1T[:, :], ALU.mult).then_inc(q["zx_done"], 1)
                if ahead:
                    k_heads(t + 1)
                    k_heads_rest(t + 1, range(1, 2))
                if l0:
                    rsqrt(0, t)
                if ahead:
                    k_heads_rest(t + 1, range(2, 3))
                if l1:
                    rsqrt(1, m)
                if ahead:
                    k_heads_rest(t + 1, range(3, H0))

            k_heads(0)
            k_heads_rest(0, range(1, H0))
            steps(pool, step)

        @block.tensor
        def _(pe):
            mm = nc.tensor.matmul

            pe.wait_ge(q["ones_set"], 1)
            pe.wait_ge(q["wcol"], 12 * DMA)
            pe.wait_ge(q["wload"], 2 * DMA)
            mm(M[:, 0, 0:NROW - 1], ones[0:1, :], row[:, 0:NROW - 1], start=True, stop=True)\
                .then_inc(q["rows_ps"], 1)
            mm(M[0:1, 1, 0:2], col[:, C_WB:C_WB + 1], col[:, C_A1:C_A2 + 1], start=True, stop=True)\
                .then_inc(q["brow_ps"], 1)
            mm(L[:, 0, 0:2], wm[:, WL2N:WL2N + N], col[:, C_A1:C_A2 + 1], start=True, stop=True)
            mm(S[0][:, 0:2 * H3], wm[:, WL3T:WL3T + N], att[:, :], start=True, stop=True).then_inc(q["wa_ps"], 1)
            pe.wait_ge(q["brow_set"], 1)
            mm(S[1][:, 0:2], ones[0:1, :], brow[:, :], start=True, stop=True).then_inc(q["bl2_ps"], 1)
            pe.wait_ge(q["prep"], 1)

            def transpose4(dst, src):
                for b in range(GB):
                    last = nc.tensor.transpose(g(dst, b), g(src, b), ident[:, :])
                return last

            def project_k(s, p, k):
                pe.wait_ge(loaded[p], (k + 1) * 3 * DMA)
                wait(pe, q["sc_ready"], 8 * s)
                wait(pe, q["pT3_ready"], H3 * (s - 4) + 1)
                mm(S[0][:, :], wm[:, WK:WK + N], xt[p][:, :], start=True, stop=True).then_inc(q["k_ps"], 1)

            def project_q(s, p):
                wait(pe, q["sc_ready"], 8 * s)
                wait(pe, q["pT3_ready"], H3 * (s - 3))
                mm(S[1][:, :], wm[:, WQ:WQ + N], xt[p][:, :], start=True, stop=True).then_inc(q["q_ps"], 1)

            def project_v(s, p):
                wait(pe, q["res0_done"], s)
                for b in range(GB):
                    last = mm(g(T, b), g(xt[p], b), wm[:, WV:WV + N], start=True, stop=True)
                last.then_inc(q["v_ps"], 1)

            def scores(s, h):
                if h == 0:
                    pe.wait_ge(q["mask0_ready"], s + 1)
                    pe.wait_ge(q["qT_ready"], s + 1)
                pe.wait_ge(q["kh_ready"], 8 * s + h + 1)
                wait(pe, q["sc_ready"], 8 * s + h - 1)
                mm(S[h % 2][:, :], identb[:, :], mask0[:, :], start=True, stop=False, skip_group_check=True)
                for b in range(GB):
                    last = mm(g(S[h % 2], b), g(qT, b), g(kh[:, h, :], b), start=False, stop=True,
                              skip_group_check=True)
                last.then_inc(q["qk_ps"], 1)

            def probs_T(s, h):
                pe.wait_ge(q["p_ready"], 8 * s + h + 1)
                wait(pe, q["pT_ready"], 8 * s + h)
                if h == 0:
                    pe.wait_ge(q["v_ready"], s + 1)
                    wait(pe, q["h3_ready"], s - 2)
                transpose4(T, p0[:, h % 2, :]).then_inc(q["tr_ps"], 1)

            def values(s, h):
                pe.wait_ge(q["pT_ready"], 8 * s + h + 1)
                if h == 0:
                    wait(pe, q["oT_ready"], s)
                    wait(pe, q["ej_ready"], s - 2)
                r = slice(32 * (h // 2), 32 * (h // 2) + 32)
                for b in range(GB):
                    c = (b * H0 + h) * 32
                    last = mm(O[r, b * N:(b + 1) * N], vpad[:, c:c + 32], g(pT0[:, h % 2, :], b),
                              start=(h % 2 == 0 and b == 0), stop=(h % 2 == 1), skip_group_check=True)
                last.then_inc(q["pv_ps"], 1)

            def project_out(s):
                pe.wait_ge(q["oT_ready"], s + 1)
                for b in range(GB):
                    last = mm(g(T, b), g(oT, b), wm[:, WO:WO + N], start=True, stop=True)
                last.then_inc(q["wo_ps"], 1)

            def tap(t):
                return wm[:, WC2 + t * N:WC2 + (t + 1) * N]

            def products(bank, slot, src, weights, start=False):
                for c, w in enumerate(weights):
                    last = mm(phases(M[:, bank, :])[:, slot], w,
                              src[:, :, c:c + Q], start=(start and c == 0), stop=True, skip_group_check=True)
                return last

            def conv(m, i):
                ws = [[wsum[:, j, c, :] for c in range(4)] for j in range(5)]
                if i == 2:
                    pe.wait_ge(q["hp_ready"], m + 1)
                    products(1, 2, xs[:, 5], ws[2] + [tap(16)], start=True)
                    products(1, 3, xs[:, 5], ws[2] + [tap(16)])
                if i == 3:
                    pe.wait_ge(q["x2_ready"], m + 1)
                    products(1, 0, xs[:, 3], ws[4])
                    products(1, 2, xd[:, 2], ws[0] + [tap(16)])
                    products(1, 3, xf[:, 2], ws[1])
                if i == 4:
                    products(1, 1, xs[:, 1], ws[3] + [tap(16)]).then_inc(q["cp_ps"], 1)
                    pe.wait_ge(q["em_ready"], m + 1)
                    products(0, 0, xd[:, 1], [tap(4 * c + 1) for c in range(4)], start=True)
                if i == 5:
                    products(0, 1, xf[:, 1], [tap(4 * c + 3) for c in range(4)])
                    products(0, 2, xd[:, 0], [tap(4 * c) for c in range(5)])
                if i == 6:
                    products(0, 3, xf[:, 0], [tap(4 * c + 2) for c in range(4)]).then_inc(q["c2_ps"], 1)

            def gate(bank, j, parts, done, first=True):
                for n, (w, src) in enumerate(parts):
                    last = mm(M[:, bank, :], wm[:, w + j * N:w + (j + 1) * N], src[:, :],
                              start=(first and n == 0), stop=(done is not None and n == len(parts) - 1))
                if done is not None:
                    last.then_inc(q[done], 1)

            def gates_with_conv(m):
                pe.wait_ge(q["xc_ready"], m + 1)
                gate(1, 0, [(WIC, xcT)], "r_ps", first=False)
                gate(0, 1, [(WIC, xcT)], "z_ps", first=False)

            def layer1(m, i):
                if i == 0:
                    pe.wait_ge(ln_out[0], m + 1)
                    wait(pe, q["g2_done"], m)
                    transpose4(M[:, 0, :], x1).then_inc(q["x1t_ps"], 1)
                if i == 1:
                    pe.wait_ge(q["x1T_ready"], m + 1)
                    wait(pe, ln_out[1], m)
                    mm(M[:, 1, :], wm[:, W1:W1 + N], x1T[:, :], start=True, stop=True).then_inc(q["c1_ps"], 1)
                    mm(M[0:KS, 0, :], wse_s[:, :], x1T[:, :], start=True, stop=True).then_inc(q["d_ps"], 1)
                if i == 3:
                    pe.wait_ge(q["lr_done"], m + 1)
                    pe.wait_ge(q["m1_done"], m + 1)
                    for b in range(GB):
                        last = mm(g(M[:, 0, :], b), g(ll, b), g(lr, b), start=True, stop=True)
                    last.then_inc(q["arg_ps"], 1)
                conv(m, i)
                if i == 2:
                    pe.wait_ge(q["dd_ready"], m + 1)
                    for b in range(GB):
                        last = mm(g(M[:, 0, :], b), g(x1T, b), wm[:, WM:WM + N], start=True, stop=True)
                    last.then_inc(q["msg_ps"], 1)
                if i == 6:
                    pe.wait_ge(q["aT_done"], m + 1)
                    pe.wait_ge(q["msg_ready"], m + 1)
                    pe.wait_ge(q["v2_done"], m + 1)
                    for b in range(GB):
                        last = mm(g(M[:, 1, :], b), g(msg, b), g(aT, b), start=True, stop=True)
                    last.then_inc(q["nmp_ps"], 1)
                if i == 7:
                    pe.wait_ge(q["nmT_ready"], m + 1)
                    gate(1, 0, [(WHH, x1T), (WIN, nmT)], None)
                if i == 8:
                    pe.wait_ge(q["u_done"], m + 1)
                    gate(0, 1, [(WHH, x1T), (WIN, nmT)], None)
                if i == 9:
                    pe.wait_ge(q["tr_ready"], m + 1)
                    gate(1, 2, [(WHH, x1T)], "ghn_ps")
                    pe.wait_ge(q["tz_ready"], m + 1)
                    gate(0, 2, [(WIC, xcT), (WIN, nmT)], "gin_ps")
                if i == 12:
                    pe.wait_ge(q["y_done"], m + 1)
                    transpose4(M[:, 1, :], yT).then_inc(q["yt_ps"], 1)

            def layer2(u, i, p):
                if i == 1:
                    pe.wait_ge(ln_out[1], u + 1)
                    wait(pe, q["o3T_ready"], u - 1)
                    transpose4(L[:, 1, :], x2).then_inc(q["x2t_ps"], 1)
                if i == 2:
                    pe.wait_ge(q["x2T_ready"], u + 1)
                    wait(pe, q["r3_done"], u - 1)
                    for b in range(GB):
                        c = (b % 2) * HC
                        last = mm(L[:, b // 2, c:c + HC], g(x2T, b), l2w[:, :], start=True, stop=True)
                    last.then_inc(q["h2_ps"], 1)
                if i == 4:
                    pe.wait_ge(q["hg_done"], u + 1)
                    for b in range(GB):
                        c = (b % 2) * HC
                        last = mm(L[:, b // 2, c:c + HC], g(at[p], b), hg[:, b, :], start=True, stop=True)
                    last.then_inc(q["num_ps"], 1)

            def layer3(t, u, i, p, l0, l2):
                if i == 0:
                    pe.wait_ge(ln_out[2], u + 1)
                    wait(pe, q["oT_ready"], min(t, GROUPS) if isinstance(t, int) else t)
                    transpose4(O, x3[p]).then_inc(q["x3t_ps"], 1)
                if i == 1:
                    pe.wait_ge(q["x3T_ready"], u + 1)
                    if l0:
                        pe.wait_ge(q["v_ready"], t + 1)
                    else:
                        pe.wait_ge(q["res0_done"], GROUPS)
                    for b in range(GB):
                        dst = O[:, b * GC:(b + 1) * GC] if b < GB - 1 else T[:, 0:GC]
                        last = mm(dst, g(x3T, b), l3w[:, :], start=True, stop=True)
                    last.then_inc(q["h3_ps"], 1)
                if i == 2:
                    pe.wait_ge(q["h3_ready"], u + 1)
                    mm(O[0:96, :], wa2[:, :], x3T[:, :], start=True, stop=True).then_inc(q["ej_ps"], 1)
                for h in {5: (0, 1), 6: (2,), 7: (3,)}.get(i, ()):
                    if h == 0:
                        pe.wait_ge(q["h3_ready"], u + 1)
                        pe.wait_ge(q["mask3_kept"], u + 1)
                        pe.wait_ge(q["ej_split"], u + 1)
                        if l2:
                            pe.wait_ge(q["r2_done"], u + 2)
                        else:
                            pe.wait_ge(q["r3_done"], u)
                    if h >= 2:
                        pe.wait_ge(q["z3_ready"], H3 * u + h - 1)
                    mm(L[:, h % 2, :], seljb[:, h, :], ejb[:, :], start=True, stop=False)
                    mm(L[:, h % 2, :], identb[:, :], mask3_late[:, :], start=False, stop=True)\
                        .then_inc(q["e3_ps"], 1)

            def layer3_T(t, u, i, l0):
                if 8 <= i < 8 + H3:
                    h = i - 8
                    pe.wait_ge(q["p3_ready"], H3 * u + h + 1)
                    if l0 and h == 0:
                        pe.wait_ge(q["sc_ready"], H0 * t + H0)
                    if h >= 2:
                        pe.wait_ge(q["pT3_ready"], H3 * u + h)
                    transpose4(S[min(h, 1)], p3[:, h % 2, :]).then_inc(q["tr3_ps"], 1)

            def layer3_values(u, i):
                if 9 <= i < 9 + H3:
                    h = i - 9
                    if h == 0:
                        pe.wait_ge(q["z3_ready"], H3 * u + H3)
                    pe.wait_ge(q["pT3_ready"], H3 * u + h + 1)
                    for b in range(GB):
                        last = mm(L[32 * h:32 * h + 32, 1, b * N:(b + 1) * N], h3[:, b, h * D3:(h + 1) * D3],
                                  g(pT3[:, h % 2, :], b), start=(b == 0), stop=True, skip_group_check=True)
                    last.then_inc(q["pv3_ps"], 1)

            def layer3_out(u):
                pe.wait_ge(q["o3T_ready"], u + 1)
                pe.wait_ge(q["z3_ready"], H3 * u + H3)
                transpose4(L[:, 0, :], o3T).then_inc(q["o3n_ps"], 1)

            def step(k, p, phases_now):
                l0, l1, l2, l3, l3e, ahead = phases_now
                t = 2 * k + p
                for i in range(SLOTS):
                    if l3e and i == 0:
                        layer3_out(t - 4)
                    if l0 and i == 0:
                        project_v(t, p)
                    if l0 and 0 <= i < H0:
                        scores(t, i)
                    if l2 and i == 4:
                        layer2(t - 2, i, p)
                    if l1 and i not in (0, 7):
                        layer1(t - 1, i)
                    if l0 and 0 <= i - 3 < H0 and i not in (7, 8):
                        values(t, i - 3)
                    if l3:
                        layer3(t, t - 3, i, 1 - p, l0, l2)
                    if l0 and i == 7:
                        values(t, i - 3)
                    if l1 and i in (0, 7):
                        layer1(t - 1, i)
                    if l1 and i == 8:
                        gates_with_conv(t - 1)
                    if l0 and i == 8:
                        values(t, i - 3)
                    if l2 and i != 4:
                        layer2(t - 2, i, p)
                    if l0 and 0 <= i - 2 < H0:
                        probs_T(t, i - 2)
                    if ahead and i == H0 + 3:
                        project_k(t + 1, 1 - p, k + p)
                    if l3:
                        layer3_T(t, t - 3, i, l0)
                    if l0 and i == H0 + 3:
                        project_out(t)
                    if l3:
                        layer3_values(t - 3, i)
                    if ahead:
                        if i == SLOTS - 2:
                            project_q(t + 1, 1 - p)

            project_k(0, 0, 0)
            project_q(0, 0)
            steps(pe, step)

        @block.scalar
        def _(act):
            fn = nc.scalar.activation

            def project_k(s):
                act.wait_ge(q["k_ps"], s + 1)
                wait(act, q["kh_ready"], 8 * s)
                fn(kT[:, :], S[0][:, :], ACT.Copy).then_inc(q["kT_ready"], 1)

            def project_q(s):
                act.wait_ge(q["q_ps"], s + 1)
                wait(act, q["qk_ps"], 8 * s)
                fn(qT[:, :], S[1][:, :], ACT.Copy, scale=float(D0) ** -0.5).then_inc(q["qT_ready"], 1)

            def project_v(s):
                act.wait_ge(q["v_ps"], s + 1)
                wait(act, q["pv_ps"], 8 * s)
                src = T[:, :].rearrange("p (m e d) -> p m e d", e=2, d=D0)
                dst = vpad[:, :].rearrange("p (m e f d) -> p m e f d", e=2, f=2, d=D0)
                fn(dst[:, :, 0, 0, :], src[:, :, 0, :], ACT.Copy)
                fn(dst[:, :, 1, 1, :], src[:, :, 1, :], ACT.Copy).then_inc(q["v_ready"], 1)

            def exps(s, h):
                act.wait_ge(q["nm_ready"], 8 * s + h + 1)
                wait(act, q["p_ready"], 8 * s + h - 1)
                for b in range(GB):
                    last = fn(g(e0[:, h % 2, :], b), g(sc0[:, h % 2, :], b), ACT.Exp, bias=nm0[:, h % 2, b:b + 1],
                              accum_out=sum0[:, h % 2, b:b + 1])
                last.then_inc(q["exp_done"], 1)

            def probs_T(s, h):
                act.wait_ge(q["tr_ps"], 8 * s + h + 1)
                wait(act, q["pv_ps"], 8 * s + h - 1)
                fn(pT0[:, h % 2, :], T[:, :], ACT.Copy).then_inc(q["pT_ready"], 1)

            def layer1(m, i):
                if i == 0:
                    act.wait_ge(q["x1t_ps"], m + 1)
                    wait(act, q["y_done"], m)
                    fn(x1T[:, :], M[:, 0, :], ACT.Copy).then_inc(q["x1T_ready"], 1)
                if i == 1:
                    act.wait_ge(q["c1_ps"], m + 1)
                    wait(act, q["c2_ps"], m)
                    fn(xs[:, 4:8, :, PAD // 4:PAD // 4 + Q],
                       phases(M[:, 1, :]), ACT.Relu, bias=bnb[:, 0:1], scale=bns[:, 0:1])\
                        .then_inc(q["hp_ready"], 1)
                    act.wait_ge(q["d_ps"], m + 1)
                    wait(act, q["lr_done"], m)
                    fn(dd[:, :], M[0:KS, 0, :], ACT.Identity, bias=bse_s[:, :]).then_inc(q["dd_ready"], 1)
                if i == 2:
                    act.wait_ge(q["dd_ready"], m + 1)
                    fn(sql[:, :], dd[:, :], ACT.Square, scale=sel[:, 2:3], bias=sel[:, 1:2])
                    fn(sqr[:, :], dd[:, :], ACT.Square, scale=sel[:, 1:2], bias=sel[:, 2:3])\
                        .then_inc(q["sq_ready"], 1)
                    act.wait_ge(q["m1_done"], m + 1)
                    fn(msg[:, :], msg[:, :], ACT.Relu).then_inc(q["msg_ready"], 1)
                if i == 3:
                    act.wait_ge(q["arg_ps"], m + 1)
                    wait(act, q["aT_done"], m)
                    fn(em[:, :], M[:, 0, :], ACT.Exp).then_inc(q["em_ready"], 1)
                if i == 6:
                    act.wait_ge(q["nmp_ps"], m + 1)
                    wait(act, q["gin_ps"], m)
                    fn(nmT[:, :], M[:, 1, :], ACT.Copy).then_inc(q["nmT_ready"], 1)
                if i == 7:
                    act.wait_ge(q["u_done"], m + 1)
                    fn(xcT[:, :], u1[:, :], ACT.Relu, bias=bnb[:, 1:2]).then_inc(q["xc_ready"], 1)
                if i == 8:
                    act.wait_ge(q["r_ps"], m + 1)
                    wait(act, q["rr_done"], m)
                    fn(tr[:, :], M[:, 1, :], ACT.Tanh, bias=gb[:, 0:1], scale=0.5).then_inc(q["tr_ready"], 1)
                    act.wait_ge(q["z_ps"], m + 1)
                    wait(act, q["zp_done"], 2 * m)
                    fn(tz[:, :], M[:, 0, :], ACT.Tanh, bias=gb[:, 1:2], scale=0.5).then_inc(q["tz_ready"], 1)
                if i == 10:
                    act.wait_ge(q["g2_done"], m + 1)
                    wait(act, q["zn_done"], m)
                    fn(nT[:, :], gn[:, :], ACT.Tanh, bias=col[:, C_BIN:C_BIN + 1]).then_inc(q["n_ready"], 1)

            def layer2(u, i):
                if i == 1:
                    act.wait_ge(q["x2t_ps"], u + 1)
                    wait(act, q["h2_ps"], u)
                    fn(x2T[:, :], L[:, 1, :], ACT.Copy).then_inc(q["x2T_ready"], 1)
                if i == 2:
                    act.wait_ge(q["hb_done"], u + 1)
                    wait(act, q["wr_done"], u)
                    fn(eg[:, :, :], h2[:, :, N:HC], ACT.Exp).then_inc(q["eg_ready"], 1)

            def layer3(u, i):
                if i == 0:
                    act.wait_ge(q["x3t_ps"], u + 1)
                    wait(act, q["ej_ps"], u)
                    fn(x3T[:, :], O[:, :], ACT.Copy).then_inc(q["x3T_ready"], 1)
                if i == 1:
                    act.wait_ge(q["h3_ps"], u + 1)
                    wait(act, q["pv3_ps"], H3 * u)
                    fn(h3[:, 0:GB - 1, :].rearrange("p b c -> p (b c)"), O[:, 0:(GB - 1) * GC], ACT.Copy)
                    fn(h3[:, GB - 1, :], T[:, 0:GC], ACT.Copy).then_inc(q["h3_ready"], 1)
                if i == 2:
                    act.wait_ge(q["ej_ps"], u + 1)
                    wait(act, q["ej_split"], u)
                    fn(ej[:, :], O[0:96, :], ACT.Copy)
                    wait(act, q["e3_ps"], H3 * u)
                    fn(ejb[:, :], O[0:96, :], ACT.Copy).then_inc(q["ej_ready"], 1)
                if 6 <= i < 6 + H3:
                    h = i - 6
                    act.wait_ge(q["nm3_ready"], H3 * u + h + 1)
                    wait(act, q["p3_ready"], H3 * u + h - 1)
                    for b in range(GB):
                        last = fn(g(e3[:, h % 2, :], b), g(l3[:, h % 2, :], b), ACT.Exp,
                                  bias=nm3[:, h % 2, b:b + 1], accum_out=sum3[:, h % 2, b:b + 1])
                    last.then_inc(q["exp3_done"], 1)
                for h in {5: (0,), 6: (1, 2), 7: (3,)}.get(i, ()):
                    if h == 0:
                        act.wait_ge(q["h3_ready"], u + 1)
                    act.wait_ge(q["e3_ps"], H3 * u + h + 1)
                    wait(act, q["l3_done"], H3 * u + h - 1)
                    for b in range(GB):
                        last = fn(g(z3[:, h % 2, :], b), g(L[:, h % 2, :], b), ACT.Identity,
                                  bias=h3[:, b, N + h:N + h + 1])
                    last.then_inc(q["z3_ready"], 1)

            def layer3_T(u, i):
                if 8 <= i < 8 + H3:
                    h = i - 8
                    act.wait_ge(q["tr3_ps"], H3 * u + h + 1)
                    wait(act, q["pv3_ps"], H3 * u + h - 1)
                    fn(pT3[:, h % 2, :], S[min(h, 1)][:, :], ACT.Copy).then_inc(q["pT3_ready"], 1)

            act.wait_ge(q["prep"], 1)

            def step(k, p, phases_now):
                l0, l1, l2, l3, l3e, ahead = phases_now
                t = 2 * k + p
                for i in range(SLOTS):
                    if l0:
                        if 0 <= i - 1 < H0:
                            exps(t, i - 1)
                        if i == H0 + 3:
                            act.wait_ge(q["pv_ps"], 8 * t + 8)
                            wait(act, q["wo_ps"], t)
                            fn(oT[:, :], O[:, :], ACT.Copy).then_inc(q["oT_ready"], 1)
                    if l0 and i == 0:
                        project_v(t)
                    if l1 and i in (1, 2, 7, 8):
                        layer1(t - 1, i)
                    if l0 and i == H0 + 1:
                        probs_T(t, i - 2)
                    if l3:
                        layer3(t - 3, i)
                    if l1 and i not in (1, 2, 7, 8):
                        layer1(t - 1, i)
                    if l2:
                        layer2(t - 2, i)
                    if l0 and 0 <= i - 2 < H0 - 1:
                        probs_T(t, i - 2)
                    if l3:
                        layer3_T(t - 3, i)
                    if l3 and i == SLOTS - 2:
                        act.wait_ge(q["pv3_ps"], H3 * (t - 3) + H3)
                        wait(act, q["o3n_ps"], t - 3)
                        fn(o3T[:, :], L[:, 1, :], ACT.Copy).then_inc(q["o3T_ready"], 1)
                    if ahead:
                        if i == SLOTS - 3:
                            project_k(t + 1)
                        if i == SLOTS - 2:
                            project_q(t + 1)

            project_k(0)
            project_q(0)
            steps(act, step)

        @block.vector
        def _(dve):
            v = nc.vector
            dve.wait_ge(q["bn2_"], 1)
            v.tensor_tensor(bns[:, 0:1], bns[:, 0:1], col[:, C_G1:C_G1 + 1], ALU.mult)
            v.tensor_tensor(bns[:, 1:2], bns[:, 1:2], col[:, C_G2:C_G2 + 1], ALU.mult).then_inc(q["bn3_"], 1)
            dve.wait_ge(q["bn3_"], 1)
            v.tensor_tensor(bnt[:, 0:1], bns[:, 0:1], col[:, C_M1:C_M1 + 1], ALU.mult)
            v.tensor_tensor(bnt[:, 1:2], bns[:, 1:2], col[:, C_M2:C_M2 + 1], ALU.mult).then_inc(q["bn3_"], 1)
            v.tensor_tensor(gb[:, :], col[:, C_BIR:C_BIZ + 1], col[:, C_BHR:C_BHZ + 1], ALU.add)\
                .then_inc(q["bn4_"], 1)
            dve.wait_ge(q["bn3_"], 2)
            v.tensor_tensor(bnb[:, 0:1], col[:, C_B1:C_B1 + 1], bnt[:, 0:1], ALU.subtract)
            v.tensor_tensor(bnb[:, 1:2], col[:, C_B2:C_B2 + 1], bnt[:, 1:2], ALU.subtract)
            dve.wait_ge(q["bn4_"], 1)
            v.tensor_scalar(gb[:, :], gb[:, :], 0.5, None, ALU.mult)
            dve.wait_ge(q["rows_ps"], 1)
            v.tensor_copy(rowb[:, 0:H0 + 2 * N], M[:, 0, 0:H0 + 2 * N])
            dve.wait_ge(q["brow_ps"], 1)
            v.tensor_copy(brow[:, :], M[0:1, 1, 0:2]).then_inc(q["bn4_"], 1)
            dve.wait_ge(q["bn4_"], 2)
            v.tensor_tensor(brow[:, 0:1], brow[:, 0:1], row[:, R_AB:R_AB + 1], ALU.add).then_inc(q["brow_set"], 1)
            dve.wait_ge(q["wa_ps"], 1)
            v.tensor_copy(l2w[:, 0:N], wm[:, WL2:WL2 + N])
            v.tensor_copy(l2w[:, N:HC], L[:, 0, 0:2])
            v.tensor_copy(l3w[:, 0:N], wm[:, WL3:WL3 + N])
            v.tensor_copy(l3w[:, N:GC], S[0][:, 0:H3])
            dve.wait_ge(q["pads_set"], 1)
            for j in range(3):
                v.tensor_copy(wa2[:, 32 * j:32 * j + H3], S[0][:, H3:2 * H3])
            dve.wait_ge(q["selj_set"], 5)
            taps = wm[:, WC2:WC2 + 16 * N].rearrange("p (c j n) -> p j c n", j=4, n=N)
            for j, (a, b) in enumerate(((0, 1), (2, 3), (None, None), (0, 2), (1, 3))):
                if a is not None:
                    last = v.tensor_tensor(wsum[:, j], taps[:, a], taps[:, b], ALU.add)
            last.then_inc(q["wsum_set"], 1)
            dve.wait_ge(q["wsum_set"], 1)
            v.tensor_tensor(wsum[:, 2], wsum[:, 0], wsum[:, 1], ALU.add)
            dve.wait_ge(q["bl2_ps"], 1)
            dve.wait_ge(q["const_set"], 4)
            v.tensor_copy(rowb[:, H0 + 2 * N:H0 + 2 * N + 2], S[1][:, 0:2]).then_inc(q["prep"], 1)
            dve.wait_ge(q["prep"], 1)

            def layer_norm(i, u, src):
                for b in range(GB):
                    last = v.bn_stats(stats[i][:, b, :], g(src, b))
                last.then_inc(ln_stats[i], 1)
                dve.wait_ge(q["prep"], 1)
                dve.wait_ge(ln_stats[i], u + 1)
                for b in range(GB):
                    last = v.bn_aggr(meanv[i][:, b, :], stats[i][:, b, :])
                last.then_inc(ln_aggr[i], 1)

            def layer_norm_end(i, u, src, dst):
                dve.wait_ge(ln_rstd[i], u + 1)
                dve.wait_ge(ln_aggr[i], u + 1)
                for b in range(GB):
                    last = v.tensor_scalar(g(dst, b), g(src, b), meanv[i][:, b, 0:1], rstd[i][:, b:b + 1],
                                           ALU.subtract, ALU.mult)
                last.then_inc(ln_out[i], 1)

            def masks(s, p, k):
                dve.wait_ge(loaded[p], (k + 1) * 3 * DMA)
                wait(dve, q["qk_ps"], 8 * s)
                v.tensor_scalar(mask0[:, :], an[p][:, :], 0.0, NEG0, ALU.is_equal, ALU.mult)\
                    .then_inc(q["mask0_ready"], 1)

            def masks3(s, p):
                wait(dve, q["mask3_kept"], s - 1)
                v.tensor_scalar(mask3[p][:, :], an[p][:, :], 0.0, NEG3, ALU.is_le, ALU.mult)\
                    .then_inc(q["mask3_ready"], 1)

            def keep_mask3(u, p):
                dve.wait_ge(q["mask3_ready"], u + 1)
                wait(dve, q["e3_ps"], H3 * u)
                v.tensor_copy(mask3_late[:, :], mask3[p][:, :]).then_inc(q["mask3_kept"], 1)

            def scores(s, h, p):
                dve.wait_ge(q["qk_ps"], 8 * s + h + 1)
                wait(dve, q["exp_done"], 8 * s + h - 1)
                v.scalar_tensor_tensor(out=sc0[:, h % 2, :], in0=an[p][:, :], scalar=we[:, h:h + 1],
                                       in1=S[h % 2][:, :], op0=ALU.mult, op1=ALU.add).then_inc(q["sc_ready"], 1)
                dve.wait_ge(q["sc_ready"], 8 * s + h + 1)
                v.tensor_reduce(nm0[:, h % 2, :], per(sc0[:, h % 2, :]), AX, ALU.max, negate=True)\
                    .then_inc(q["nm_ready"], 1)

            def norm(s, h):
                dve.wait_ge(q["exp_done"], 8 * s + h + 1)
                v.reciprocal(rec0[:, h % 2, :], sum0[:, h % 2, :]).then_inc(q["rec_done"], 1)
                dve.wait_ge(q["rec_done"], 8 * s + h + 1)
                wait(dve, q["tr_ps"], 8 * s + h - 1)
                v.tensor_tensor(per(p0[:, h % 2, :]), per(e0[:, h % 2, :]), wide(rec0[:, h % 2, :]), ALU.mult)\
                    .then_inc(q["p_ready"], 1)

            def front_end(s, p):
                dve.wait_ge(q["wo_ps"], s + 1)
                wait(dve, ln_out[0], s)
                v.tensor_tensor(r0[:, :], T[:, :], xn[p][:, :], ALU.add).then_inc(q["res0_done"], 1)
                dve.wait_ge(q["res0_done"], s + 1)
                layer_norm(0, s, r0)

            def layer1(m, i):
                if i == 2:
                    dve.wait_ge(q["msg_ps"], m + 1)
                    wait(dve, q["nmp_ps"], m)
                    v.tensor_tensor(per(msg[:, :]), per(M[:, 0, :]),
                                    bmsg.unsqueeze(1).broadcast_to([128, GB, N]), ALU.add)\
                        .then_inc(q["m1_done"], 1)
                    dve.wait_ge(q["sq_ready"], m + 1)
                    dve.wait_ge(q["dd_ready"], m + 1)
                    wait(dve, q["arg_ps"], m)
                    v.scalar_tensor_tensor(out=lr[:, :], in0=dd[:, :], scalar=sel[:, 0:1], in1=sqr[:, :],
                                           op0=ALU.mult, op1=ALU.subtract)
                    v.scalar_tensor_tensor(out=ll[:, :], in0=dd[:, :], scalar=sel2[:, 0:1], in1=sql[:, :],
                                           op0=ALU.mult, op1=ALU.add).then_inc(q["lr_done"], 1)
                if i == 9:
                    dve.wait_ge(q["tr_ready"], m + 1)
                    v.tensor_scalar(rr[:, :], tr[:, :], 0.5, 0.5, ALU.mult, ALU.add).then_inc(q["rr_done"], 1)
                if i == 10:
                    dve.wait_ge(q["rr_done"], m + 1)
                    dve.wait_ge(q["ghn_ps"], m + 1)
                    wait(dve, q["n_ready"], m)
                    v.scalar_tensor_tensor(out=gn[:, :], in0=M[:, 1, :], scalar=col[:, C_BHN:C_BHN + 1],
                                           in1=rr[:, :], op0=ALU.add, op1=ALU.mult).then_inc(q["g1_done"], 1)
                    dve.wait_ge(q["g1_done"], m + 1)
                    dve.wait_ge(q["gin_ps"], m + 1)
                    v.tensor_tensor(gn[:, :], M[:, 0, :], gn[:, :], ALU.add).then_inc(q["g2_done"], 1)
                if i == 11:
                    dve.wait_ge(q["zx_done"], m + 1)
                    dve.wait_ge(q["zp_done"], 2 * m + 2)
                    dve.wait_ge(q["n_ready"], m + 1)
                    v.tensor_tensor(zn[:, :], zminus[:, :], nT[:, :], ALU.mult).then_inc(q["zn_done"], 1)
                    dve.wait_ge(q["zn_done"], m + 1)
                    wait(dve, q["yt_ps"], m)
                    v.tensor_tensor(yT[:, :], zn[:, :], zx[:, :], ALU.add).then_inc(q["y_done"], 1)
                if i == 12:
                    dve.wait_ge(q["yt_ps"], m + 1)
                    layer_norm(1, m, M[:, 1, :])
                if i == 13:
                    wait(dve, q["x2t_ps"], m)
                    wait(dve, q["r2_done"], m)
                    layer_norm_end(1, m, M[:, 1, :], x2)

            def conv_sum(m):
                dve.wait_ge(q["c2_ps"], m + 1)
                dve.wait_ge(q["v2_done"], m + 1)
                wait(dve, q["xc_ready"], m)
                v.scalar_tensor_tensor(out=u1[:, :], in0=M[:, 0, :], scalar=bns[:, 1:2], in1=vT[:, :],
                                       op0=ALU.mult, op1=ALU.add).then_inc(q["u_done"], 1)

            def shared_products(m):
                dve.wait_ge(q["cp_ps"], m + 1)
                dve.wait_ge(q["x1T_ready"], m + 1)
                for c in range(4):
                    last = v.scalar_tensor_tensor(
                        out=phases(vT[:, :])[:, c], in0=phases(M[:, 1, :])[:, c // 2], scalar=bns[:, 1:2],
                        in1=phases(x1T[:, :])[:, c], op0=ALU.mult, op1=ALU.add)
                last.then_inc(q["v1_done"], 1)
                dve.wait_ge(q["v1_done"], m + 1)
                for x in range(2):
                    half = vT[:, :].rearrange("p (b x n) -> p x b n", b=GB, x=2)[:, x]
                    last = v.scalar_tensor_tensor(
                        out=half, in0=M[:, 1, :].rearrange("p (b x n) -> p x b n", b=GB, x=2)[:, 1],
                        scalar=bns[:, 1:2], in1=half, op0=ALU.mult, op1=ALU.add)
                last.then_inc(q["v2_done"], 1)

            def layer2(u, i, p):
                if i == 2:
                    dve.wait_ge(q["h2_ps"], u + 1)
                    wait(dve, q["hg_done"], u)
                    for a in range(2):
                        last = v.tensor_tensor(h2[:, 2 * a:2 * a + 2, :],
                                               L[:, a, 0:2 * HC].rearrange("p (b c) -> p b c", c=HC),
                                               bl2.unsqueeze(1).broadcast_to([128, 2, HC]), ALU.add)
                    last.then_inc(q["hb_done"], 1)
                if i == 3:
                    dve.wait_ge(q["hb_done"], u + 1)
                    dve.wait_ge(q["eg_ready"], u + 1)
                    wait(dve, q["num_ps"], u)
                    v.tensor_tensor(hg[:, :, 0:N], h2[:, :, 0:N], wide(eg[:, :, 1]), ALU.mult)
                    v.tensor_copy(hg[:, :, N:HC], eg[:, :, 1:2].broadcast_to([128, GB, 2])).then_inc(q["hg_done"], 1)
                if i == 4:
                    num = L[:, 0:2, 0:2 * HC].rearrange("p a (b c) -> p a b c", c=HC)
                    dve.wait_ge(q["num_ps"], u + 1)
                    v.tensor_tensor(dn[:, :].rearrange("p (a b) -> p a b", a=2), num[:, :, :, N],
                                    eg[:, :, 0].rearrange("p (a b) -> p a b", a=2), ALU.mult)\
                        .then_inc(q["dn_done"], 1)
                    dve.wait_ge(q["dn_done"], u + 1)
                    v.reciprocal(rdn[:, :], dn[:, :]).then_inc(q["rdn_done"], 1)
                    dve.wait_ge(q["rdn_done"], u + 1)
                    v.tensor_tensor(wr[:, :], rdn[:, :], eg[:, :, 0], ALU.mult).then_inc(q["wr_done"], 1)
                    dve.wait_ge(q["wr_done"], u + 1)
                    dve.wait_ge(ln_out[1], u + 1)
                    wait(dve, ln_out[2], u)
                    for b in range(GB):
                        last = v.scalar_tensor_tensor(out=g(r2, b), in0=num[:, b // 2, b % 2, 0:N],
                                                      scalar=wr[:, b:b + 1], in1=g(x2, b),
                                                      op0=ALU.mult, op1=ALU.add)
                    last.then_inc(q["r2_done"], 1)
                    dve.wait_ge(q["r2_done"], u + 1)
                    layer_norm(2, u, r2)
                if i == 5:
                    wait(dve, q["x3t_ps"], u - 1)
                    wait(dve, q["r3_done"], u - 1)
                    layer_norm_end(2, u, r2, x3[p])

            def layer3(u, i):
                if 7 <= i < 7 + H3:
                    h = i - 7
                    dve.wait_ge(q["exp3_done"], H3 * u + h + 1)
                    v.reciprocal(rec3[:, h % 2, :], sum3[:, h % 2, :]).then_inc(q["rec3_done"], 1)
                    dve.wait_ge(q["rec3_done"], H3 * u + h + 1)
                    wait(dve, q["tr3_ps"], H3 * u + h - 1)
                    v.tensor_tensor(per(p3[:, h % 2, :]), per(e3[:, h % 2, :]), wide(rec3[:, h % 2, :]),
                                    ALU.mult).then_inc(q["p3_ready"], 1)
                if 5 <= i < 5 + H3:
                    h = i - 5
                    dve.wait_ge(q["z3_ready"], H3 * u + h + 1)
                    wait(dve, q["exp3_done"], H3 * u + h - 1)
                    v.scalar_tensor_tensor(out=l3[:, h % 2, :], in0=z3[:, h % 2, :], scalar=SLOPE,
                                           in1=z3[:, h % 2, :], op0=ALU.mult, op1=ALU.max)\
                        .then_inc(q["l3_done"], 1)
                    dve.wait_ge(q["l3_done"], H3 * u + h + 1)
                    v.tensor_reduce(nm3[:, h % 2, :], per(l3[:, h % 2, :]), AX, ALU.max, negate=True)\
                        .then_inc(q["nm3_ready"], 1)

            def layer3_end(u, p, k):
                dve.wait_ge(q["o3n_ps"], u + 1)
                dve.wait_ge(ln_out[2], u + 1)
                wait(dve, ln_out[3], u)
                v.tensor_tensor(r3[:, :], L[:, 0, :], x3[p][:, :], ALU.add).then_inc(q["r3_done"], 1)
                dve.wait_ge(q["r3_done"], u + 1)
                layer_norm(3, u, r3)

            def step(k, p, phases_now):
                l0, l1, l2, l3, l3e, ahead = phases_now
                t = 2 * k + p
                for i in range(SLOTS):
                    if l0 and 0 <= i < H0:
                        scores(t, i, p)
                    if l3e:
                        if i == 1:
                            layer3_end(t - 4, p, k)
                        if i == 2:
                            wait(dve, stored[p], (k - 2) * DMA)
                            layer_norm_end(3, t - 4, r3, xo[p])
                    if l1:
                        layer1(t - 1, i)
                    if l2:
                        layer2(t - 2, i, p)
                    if l0 and i in (H0 - 1, H0):
                        norm(t, i - 1)
                    if l3:
                        layer3(t - 3, i)
                    if l0 and 0 <= i - 1 < H0 - 2:
                        norm(t, i - 1)
                    if l1 and i == 4:
                        shared_products(t - 1)
                    if l1 and i == 6:
                        conv_sum(t - 1)
                    if l0 and i == H0 + 3:
                        front_end(t, p)
                    if ahead and i == H0 + 2:
                        masks(t + 1, 1 - p, k + p)
                    if l0:
                        if i == H0 + 4:
                            wait(dve, q["x1t_ps"], t)
                            layer_norm_end(0, t, r0, x1)
                            masks3(t, p)
                    if l2 and i == H0 + 3:
                        keep_mask3(t - 2, p)

            masks(0, 0, 0)
            steps(dve, step)


SLOTS = 14


def kernel(**inputs):
    import numpy as np
    import concourse.bacc as bacc
    from concourse.bass_utils import run_bass_kernel_spmd

    i = {n: np.ascontiguousarray(a) for n, a in inputs.items()}
    flat = lambda a: np.ascontiguousarray(a.reshape(N, -1))
    wih = i["L1_gnn_w_ih"].T
    order = np.arange(N).reshape(Q, 2, 2).transpose(2, 1, 0)[::-1].reshape(N)
    x, adj = i["x"][:, order], i["adj"][:, order][:, :, order]
    mats = np.concatenate(
        [i["L0_gnn_W_q"].T, i["L0_gnn_W_k"].T, i["L0_gnn_W_v"].T, i["L0_gnn_W_o"].T,
         i["L1_gnn_conv1_w"][:, :, 0].T, i["L1_gnn_w_msg"].T, i["L2_gnn_W_w"].T, i["L2_gnn_W_w"],
         i["L3_gnn_W"], i["L3_gnn_W"].T, i["L1_gnn_w_hh"].T, wih[0:N], wih[N:2 * N],
         i["L1_gnn_conv2_w"].transpose(1, 2, 0).reshape(N, TAPS * N)], axis=1)
    bih, bhh = i["L1_gnn_b_ih"], i["L1_gnn_b_hh"]
    cols = np.stack(
        [i["L1_gnn_bn1_g"], i["L1_gnn_bn1_b"], i["L1_gnn_bn1_m"], i["L1_gnn_bn1_v"],
         i["L1_gnn_bn2_g"], i["L1_gnn_bn2_b"], i["L1_gnn_bn2_m"], i["L1_gnn_bn2_v"],
         bih[0:N], bih[N:2 * N], bih[2 * N:], bhh[0:N], bhh[N:2 * N], bhh[2 * N:],
         i["L2_gnn_a_w"][0:N], i["L2_gnn_a_w"][N:], i["L2_gnn_W_b"]], axis=1)
    rows = np.concatenate([i["L0_gnn_W_e"][:, 0], i["L1_gnn_b_msg"], i["L2_gnn_W_b"], i["L2_gnn_a_b"]])[None, :]
    arrays = {
        "x_n": flat(x.transpose(1, 0, 2)), "x_t": flat(x.transpose(2, 0, 1)),
        "adj_n": flat(adj.transpose(1, 0, 2)), "adj_t": flat(adj.transpose(2, 0, 1)),
        "mats": np.ascontiguousarray(mats),
        "wse": np.ascontiguousarray(np.concatenate([i["L1_gnn_w_se"].T] * 3, axis=1)),
        "cols": np.ascontiguousarray(cols), "rows": np.ascontiguousarray(rows),
        "bse": np.ascontiguousarray(np.concatenate([i["L1_gnn_b_se"]] * 3)[:, None]),
        "att3": i["L3_gnn_a"],
    }
    nc = bacc.Bacc("TRN2", target_bir_lowering=False, num_devices=1)
    args = [nc.dram_tensor(f"in_{n}", a.shape, F32, kind="ExternalInput").ap() for n, a in arrays.items()]
    out = nc.dram_tensor("out_x", (N, N * N), F32, kind="ExternalOutput").ap()
    build(nc, *args, out)
    r = run_bass_kernel_spmd(nc, [{f"in_{n}": a for n, a in arrays.items()}], core_ids=[0])
    return np.ascontiguousarray(r.results[0]["out_x"].reshape(N, N, N).transpose(1, 0, 2)[:, np.argsort(order)])
```
